# Optimizing a Trainium2 kernel written in Bass

```python
import numpy as np
import jax
import jax.numpy as jnp

def _softmax(x, axis=-1):
    return jax.nn.softmax(x, axis=axis)

def _gelu(x):
    return jax.nn.gelu(x, approximate=True)

def _silu(x):
    return jax.nn.silu(x)

def _sigmoid(x):
    return jax.nn.sigmoid(x)

def _layernorm(x, axis=-1, eps=1e-05):
    m = jnp.mean(x, axis=axis, keepdims=True)
    v = jnp.var(x, axis=axis, keepdims=True)
    return (x - m) / jnp.sqrt(v + eps)

def _scatter_add(tgt, idx, src, axis=0):
    return tgt.at[idx].add(src)

def _segment_sum(src, seg, n):
    return jax.ops.segment_sum(src, seg, n)
kernel_name = 'mk_xattn_ffn_d1_seqx_r4_86066b'

def setup_inputs(seed: int=0):
    np.random.seed(seed)
    _w = jnp.asarray

    def _rec_inputs():
        import jax
        import jax.numpy as jnp
        _rk = jax.random.key(seed)
        x = 7.22e-05 + 1 * jax.random.normal(jax.random.fold_in(_rk, 1), (4, 512, 512), jnp.float32)
        _lenS = 512 - jax.random.randint(jax.random.fold_in(_rk, 7), (4,), 0, max(1, 512 // 4) + 1, jnp.int32)
        _lenS2 = 512 - jax.random.randint(jax.random.fold_in(_rk, 8), (4,), 0, max(1, 512 // 4) + 1, jnp.int32)
        _ctx_1024P = jax.random.normal(jax.random.fold_in(_rk, 11), (4, 16, 256), jnp.float32)
        _ctx_1024c = jax.random.dirichlet(jax.random.fold_in(_rk, 511), 0.3 * jnp.ones((16,), jnp.float32), (4, 512))
        _ctx_1024t = jnp.einsum('bsk,bkd->bsd', _ctx_1024c, _ctx_1024P)
        _ctx_1024t = _ctx_1024t * jax.lax.rsqrt(jnp.mean(jnp.square(_ctx_1024t)) + 1e-12) * 0.953939
        ctx_1024 = 2.81802e-05 + 1.00001 * (_ctx_1024t + 0.3 * jax.random.normal(jax.random.fold_in(_rk, 611), (4, 512, 256), jnp.float32))
        return (x, ctx_1024)
    x, ctx_1024 = _rec_inputs()

    def _L0_xattn_setup():
        import jax, jax.numpy as jnp
        import numpy as np
        key = jax.random.key(seed)
        ks = jax.random.split(key, 6)
        B, L, N, C, D = (8, 128, 512, 256, 128)
        return {'teacher_logits': jax.random.normal(ks[0], (B, L, N), dtype=jnp.float32), 'teacher_features': jax.random.normal(ks[1], (B, N, C), dtype=jnp.float32), 'Wq': jax.random.normal(ks[2], (D, C), dtype=jnp.float32) * (1.0 / np.sqrt(C)), 'bq': jnp.zeros((D,), dtype=jnp.float32), 'Wk': jax.random.normal(ks[3], (D, C), dtype=jnp.float32) * (1.0 / np.sqrt(C)), 'bk': jnp.zeros((D,), dtype=jnp.float32)}
    _L0_xattn_all = _L0_xattn_setup()
    _L0_xattn_in = {k: v for k, v in _L0_xattn_all.items() if k in ('Wq', 'bq', 'Wk', 'bk')}
    del _L0_xattn_all

    def _L0_ffn_setup():
        import jax, jax.numpy as jnp
        import numpy as np
        EPS = 1e-08

        def _bit_quant(w):
            scale = jnp.maximum(jnp.mean(jnp.abs(w)), EPS)
            w_ternary = jnp.clip(jnp.round(w / scale), -1.0, 1.0)
            return w + jax.lax.stop_gradient(w_ternary - w)
        key = jax.random.key(seed)
        k = jax.random.split(key, 5)
        emb, dff = (512, 2048)
        B, S = (4, 512)
        x = jax.random.normal(k[0], (B, S, emb), dtype=jnp.float32)
        w1 = jax.random.normal(k[1], (dff, emb), dtype=jnp.float32) * 0.02
        b1 = jax.random.normal(k[2], (dff,), dtype=jnp.float32) * 0.02
        w2 = jax.random.normal(k[3], (emb, dff), dtype=jnp.float32) * 0.02
        b2 = jax.random.normal(k[4], (emb,), dtype=jnp.float32) * 0.02
        return {'x': x, 'w1': w1, 'b1': b1, 'w2': w2, 'b2': b2}
    _L0_ffn_all = _L0_ffn_setup()
    _L0_ffn_in = {k: v for k, v in _L0_ffn_all.items() if k in ('w1', 'b1', 'w2', 'b2')}
    del _L0_ffn_all
    return {'x': x, 'ctx_1024': ctx_1024, 'L0_xattn_Wq': _L0_xattn_in['Wq'], 'L0_xattn_bq': _L0_xattn_in['bq'], 'L0_xattn_Wk': _L0_xattn_in['Wk'], 'L0_xattn_bk': _L0_xattn_in['bk'], 'L0_ffn_w1': _L0_ffn_in['w1'], 'L0_ffn_b1': _L0_ffn_in['b1'], 'L0_ffn_w2': _L0_ffn_in['w2'], 'L0_ffn_b2': _L0_ffn_in['b2']}

def reference(x, ctx_1024, L0_xattn_Wq, L0_xattn_bq, L0_xattn_Wk, L0_xattn_bk, L0_ffn_w1, L0_ffn_b1, L0_ffn_w2, L0_ffn_b2):
    import jax
    import jax.numpy as jnp

    def _L0_xattn_ref(teacher_logits, teacher_features, Wq, bq, Wk, bk):
        import jax, jax.numpy as jnp
        import numpy as np
        query = jnp.einsum('bnc,dc->bnd', teacher_features, Wq) + bq
        key = jnp.einsum('bnc,dc->bnd', teacher_features, Wk) + bk
        energy = jnp.einsum('bnd,bmd->bnm', query, key)
        attention = jax.nn.softmax(energy, axis=-1)
        x_m = jnp.einsum('bln,bmn->blm', teacher_logits, attention)
        return x_m

    def _L0_ffn_ref(x, w1, b1, w2, b2):
        import jax, jax.numpy as jnp
        import numpy as np
        EPS = 1e-08

        def _bit_quant(w):
            scale = jnp.maximum(jnp.mean(jnp.abs(w)), EPS)
            w_ternary = jnp.clip(jnp.round(w / scale), -1.0, 1.0)
            return w + jax.lax.stop_gradient(w_ternary - w)
        w1q = _bit_quant(w1)
        w2q = _bit_quant(w2)
        h = jnp.einsum('bsd,fd->bsf', x, w1q) + b1
        h = jax.nn.gelu(h, approximate=False)
        return jnp.einsum('bsf,df->bsd', h, w2q) + b2
    x = x + _L0_xattn_ref(_layernorm(x, axis=-1), ctx_1024, L0_xattn_Wq, L0_xattn_bq, L0_xattn_Wk, L0_xattn_bk)
    x = x + _L0_ffn_ref(_layernorm(x, axis=-1), L0_ffn_w1, L0_ffn_b1, L0_ffn_w2, L0_ffn_b2)
    return x

_drawn_inputs = setup_inputs


def setup_inputs(seed=0):
    import zlib

    import numpy as np

    out = dict(_drawn_inputs(seed))
    spreads = {'L0_xattn_bq': (0.0, 0.1), 'L0_xattn_bk': (0.0, 2.0)}
    factors = {'L0_ffn_b1': 57.884, 'L0_ffn_b2': 64.0}
    for name, (base, spread) in spreads.items():
        noise = np.random.default_rng([zlib.crc32(name.encode()), seed]).standard_normal(out[name].shape)
        drawn = base * np.exp(spread * noise) if base else spread * noise
        out[name] = jnp.asarray(drawn.astype(out[name].dtype))
    for name, factor in factors.items():
        out[name] = (out[name] * factor).astype(out[name].dtype)
    return out
```

```python
from contextlib import ExitStack

import concourse.bass as bass
from concourse import mybir
from concourse.alu_op_type import AluOpType as ALU

ACT = mybir.ActivationFunctionType
AX = mybir.AxisListType
F32 = mybir.dt.float32
F16 = mybir.dt.float16
BF16 = mybir.dt.bfloat16
U8 = mybir.dt.uint8
I32 = mybir.dt.int32

LN_SCALE = 2.0 ** 10
PROB_SCALE = 2.0 ** 15
HIDDEN_TOP = 2.0 ** 14
LN_EPS = 1e-5
QUANT_EPS = 1e-8


def xattn_ffn(nc, x, ctx_in, Wq, bq, Wk, bk, w1, b1, w2, b2, out):
    B, L, D = x.shape
    C = ctx_in.shape[2]
    H = Wq.shape[0]
    F = w1.shape[0]
    P = 128
    NT = L // P
    NC = C // P
    ND = D // P
    NF = F // P
    Q = 4
    R = P // Q
    NCH = 8
    WN = F * D // P
    CH = WN // NCH
    assert ctx_in.shape[1] == L and D == L and H == P and D == ND * P

    with ExitStack() as stack:
        def sb(name, shape, dt=F32):
            return stack.enter_context(nc.sbuf_tensor(name, shape, dt))

        def sem(name):
            return stack.enter_context(nc.semaphore(name))

        x_sb = sb("x_sb", [P, B, NT, D])
        w1_raw = sb("w1_raw", [P, F // R, P])
        w2_raw = sb("w2_raw", [P, D // R, F // Q])
        w1T = sb("w1T", [P, NF, ND, P], F16)
        x2T = sb("x2T", [P, 2, B, ND, L], F16)
        scratch = sb("scratch", [P, 2, NT, D])
        probs = scratch[:, 0]
        xn = scratch[:, 1]
        x2n = sb("x2n", [P, NT, ND, P])
        W_raw = x2n[:, 0:2].rearrange("p a b c -> p a (b c)")[:, :, 0:C]
        ctx_sb = sb("ctx_sb", [P, NT, C])
        ctxT = sb("ctxT", [P, NC, L])
        qkT = sb("qkT", [P, 2, L])
        WT = sb("WT", [P, 2, NC, H])
        xnT = sb("xnT", [P, 2, ND, L], F16)
        probsT = sb("probsT", [P, 2, NT, L], F16)
        is_low = sb("is_low", [P, CH], F16)
        tern = sb("tern", [P, CH], F16)
        abs_out = sb("abs_out", [P, CH], U8)
        b2_sb = sb("b2_sb", [P, D])
        ident = sb("ident", [P, P])
        b1_rows = sb("b1_rows", [NF, P])
        b1_col = sb("b1_col", [P, NF])
        bqk = sb("bqk", [P, 2])
        h_scale = sb("h_scale", [P, NF])
        h_unscale = sb("h_unscale", [P, NF])
        bound = sb("bound", [P, NF])
        abs_sum = sb("abs_sum", [P, 2, NCH])
        abs_row = sb("abs_row", [P, 2])
        abs_all = sb("abs_all", [P, 2])
        cut = sb("cut", [P, 2, 2])
        stats = sb("stats", [P, NT, 6])
        mv = sb("mv", [P, NT, 2])
        var_eps = sb("var_eps", [P, NT])
        rstd = sb("rstd", [P, NT])
        stats2 = sb("stats2", [P, NT, 6])
        mv2 = sb("mv2", [P, NT, 2])
        var_eps2 = sb("var_eps2", [P, NT])
        rstd2 = sb("rstd2", [P, NT])
        minus_half = sb("minus_half", [P, NT])
        row_max = sb("row_max", [P, NT])
        row_sum = sb("row_sum", [P, NT])
        row_inv = sb("row_inv", [P, NT])

        w1_flat = w1_raw[:].rearrange("p a b -> p (a b)")
        w2T = w1_flat[:, 0:WN // 2].bitcast(BF16).rearrange("p (k e) -> p k e", k=NF)
        gT_hi = w1_flat[:, WN // 2:WN].bitcast(F16).rearrange("p (k t) -> p k t", k=NF)
        gT_lo = scratch[:].rearrange("p a b c -> p (a b c)").bitcast(F16).rearrange("p (k t) -> p k t", k=NF)

        ps_t = [stack.enter_context(nc.psum_tensor(f"ps_t{i}", [P, L], F32)) for i in range(4)]
        ps_e = [stack.enter_context(nc.psum_tensor(f"ps_e{i}", [P, L], F32)) for i in range(4)]

        small_in = sem("small_in")
        ctx_here = sem("ctx_here")
        x_here = sem("x_here")
        w_here = [[sem(f"w{m + 1}_here{h}") for h in range(2)] for m in range(2)]
        out_done = sem("out_done")
        ident_zero, ident_done = sem("ident_zero"), sem("ident_done")
        var_eps_done, rstd_done = sem("var_eps_done"), sem("rstd_done")
        var_eps2_done, rstd2_done = sem("var_eps2_done"), sem("rstd2_done")
        probs_done = sem("probs_done")
        b2_added = sem("b2_added")
        abs_all_done = sem("abs_all_done")
        WT_ready, b1T_ready = sem("WT_ready"), sem("b1T_ready")
        ctxT_ready, qk_ready, scores_ready = sem("ctxT_ready"), sem("qk_ready"), sem("scores_ready")
        xnT_ready, probsT_ready, attn_ready = sem("xnT_ready"), sem("probsT_ready"), sem("attn_ready")
        x2T_ready, hidden_ready, y_ready = sem("x2T_ready"), sem("hidden_ready"), sem("y_ready")
        exp_done, abs_done = sem("exp_done"), sem("abs_done")
        probsT_hi_done, xnT_hi_done, x2T_hi_done = sem("probsT_hi_done"), sem("xnT_hi_done"), sem("x2T_hi_done")
        gelu_done, gT_hi_done = sem("gelu_done"), sem("gT_hi_done")
        stats_done, mv_done, xn_done = sem("stats_done"), sem("mv_done"), sem("xn_done")
        stats2_done, mv2_done, x2n_done = sem("stats2_done"), sem("mv2_done"), sem("x2n_done")
        max_done, inv_done, x2_done, y_done = sem("max_done"), sem("inv_done"), sem("x2_done"), sem("y_done")
        abs_row_done, cut_half, cut_done = sem("abs_row_done"), sem("cut_half"), sem("cut_done")
        is_low_done, tern_done, turned_done = sem("is_low_done"), sem("tern_done"), sem("turned_done")
        bound_step, h_scale_done, w2T_done = sem("bound_step"), sem("h_scale_done"), sem("w2T_done")
        minus_half_done = sem("minus_half_done")
        bank_read = [sem(f"bank_read{j}") for j in range(4)]

        LAST = B - 1

        def before_step(b, j):
            if isinstance(b, int) and b == 0:
                return 1 if j < 2 else 2
            return 4 * b + (0 if j < 2 else 1)

        def n_ctx(b, j):
            return before_step(b, j)

        def n_probs(b, j, last=False):
            return before_step(b, j) + (1 if j < 2 and not last else 0)

        def n_qk(b, s):
            return before_step(b, 2 + s) + 1

        def n_xn(b, j, last=False):
            return before_step(b, j) + (1 if last else 2)

        def n_x2(b, j, last=False):
            return before_step(b, j) + (2 if last else 3)

        AFTER_A = [before_step(LAST, j) + 3 for j in range(4)]
        GROUPS = NF // 4

        def n_hidden(b, g, j):
            first = isinstance(b, int) and b == 0
            return AFTER_A[j] + g if first else AFTER_A[j] + GROUPS * b + 1 + g

        N_X2_LAST = [AFTER_A[j] + GROUPS for j in range(4)]

        x_tiles = x.rearrange("b (t p) d -> b p t d", p=P)
        ctx_tiles = ctx_in.rearrange("b (t p) c -> b p t c", p=P)
        out_tiles = out.rearrange("b (t p) d -> b p t d", p=P)
        w_views = [w1.rearrange("(fb r) (q d) -> q r fb d", r=R, q=Q), w2.rearrange("(eb r) (q f) -> q r eb f", r=R, q=Q)]
        b1_view = b1.rearrange("(q k c) -> k q c", q=Q, k=NF)
        raws = [w1_raw, w2_raw]

        block = stack.enter_context(nc.Block())

        @block.sync
        def _(sp):
            sp.dma_start(ctx_sb[:], ctx_tiles[0]).then_inc(ctx_here, 16)
            sp.dma_start(W_raw[:, 0, :], Wq).then_inc(small_in, 16)
            sp.dma_start(W_raw[:, 1, :], Wk).then_inc(small_in, 16)
            sp.dma_start(bqk[:, 0:1], bq.rearrange("(p a) -> p a", a=1)).then_inc(small_in, 16)
            sp.dma_start(bqk[:, 1:2], bk.rearrange("(p a) -> p a", a=1)).then_inc(small_in, 16)
            sp.dma_start(x_sb[:, 0], x_tiles[0]).then_inc(x_here, 16)
            sp.dma_start(b1_rows[:].rearrange("k (q c) -> k q c", q=Q), b1_view).then_inc(small_in, 16)
            sp.dma_start(b2_sb[:], b2.rearrange("(a d) -> a d", a=1).to_broadcast([P, D])).then_inc(small_in, 16)
            with sp.Fori(1, B) as b:
                sp.wait_ge(ctxT_ready, NC * b)
                sp.dma_start(ctx_sb[:], ctx_tiles[b]).then_inc(ctx_here, 16)
                sp.wait_ge(x_here, 16 * b)
                sp.dma_start(x_sb[:, b], x_tiles[b]).then_inc(x_here, 16)
            with sp.Fori(0, B) as b:
                for t in range(NT):
                    sp.wait_ge(y_done, NT * b + t + 1)
                    sp.dma_start(out_tiles[b, :, t], x_sb[:, b, t]).then_inc(out_done, 16)
            sp.wait_ge(out_done, 16 * B * NT)

        @block.gpsimd
        def _(pool):
            def rstd_of(b, mv_t, ready, ve, ve_done, r, r_done):
                pool.wait_ge(ready, NT * b + NT)
                nc.gpsimd.tensor_scalar(ve[:], mv_t[:, :, 1], LN_EPS, None, ALU.add).then_inc(ve_done, 1)
                pool.wait_ge(ve_done, b + 1)
                nc.gpsimd.tensor_tensor(r[:], ve[:], minus_half[:], ALU.pow).then_inc(r_done, 1)

            def normalise_probs(b):
                for t in range(NT):
                    pool.wait_ge(inv_done, NT * b + t + 1)
                    nc.gpsimd.tensor_scalar(probs[:, t], probs[:, t], row_inv[:, t:t + 1], PROB_SCALE,
                                            ALU.mult, ALU.mult).then_inc(probs_done, 1)

            def add_b2(b):
                for t in range(NT):
                    pool.wait_ge(x2n_done, NT * b + t + 1)
                    nc.gpsimd.tensor_tensor(x_sb[:, b, t], x_sb[:, b, t], b2_sb[:], ALU.add).then_inc(b2_added, 1)

            def weight_total(m):
                pool.wait_ge(abs_row_done, m + 1)
                nc.gpsimd.partition_all_reduce(abs_all[:, m:m + 1], abs_row[:, m:m + 1], P,
                                               bass.bass_isa.ReduceOp.add).then_inc(abs_all_done, 1)

            def step(b, last=False):
                if not last:
                    normalise_probs(b + 1)
                    rstd_of(b + 1, mv, mv_done, var_eps, var_eps_done, rstd, rstd_done)
                rstd_of(b, mv2, mv2_done, var_eps2, var_eps2_done, rstd2, rstd2_done)
                add_b2(b)

            nc.gpsimd.memset(ident[:], 0.0).then_inc(ident_zero, 1)
            pool.wait_ge(ident_zero, 1)
            nc.gpsimd.affine_select(out=ident[:], in_=ident[:], compare_op=ALU.not_equal, fill=1.0, base=0,
                                    pattern=[[-1, P]], channel_multiplier=1).then_inc(ident_done, 1)
            pool.wait_ge(minus_half_done, 1)
            rstd_of(0, mv, mv_done, var_eps, var_eps_done, rstd, rstd_done)
            normalise_probs(0)
            pool.wait_ge(small_in, 16 * 6)
            step(0)
            weight_total(0)
            for b in range(1, LAST):
                step(b)
            weight_total(1)
            step(LAST, last=True)

        @block.tensor
        def _(pe):
            def turn_ctx(b, n):
                pe.wait_ge(ctx_here, 16 * b + 16)
                for k in range(NC):
                    n(k)
                    for t in range(NT):
                        mm = nc.tensor.transpose(ps_t[k][:, t * P:(t + 1) * P], ctx_sb[:, t, k * P:(k + 1) * P], ident[:])
                    mm.then_inc(ctxT_ready, 1)

            def project(n_ctxT, n):
                for s in range(2):
                    n(s)
                    for k in range(NC):
                        if s == 0:
                            pe.wait_ge(bank_read[k], n_ctxT(k) + 1)
                        mm = nc.tensor.matmul(ps_t[2 + s][:], WT[:, s, k], ctxT[:, k], start=(k == 0), stop=(k == NC - 1))
                    mm.then_inc(qk_ready, 1)

            def scores(n_qkT, free=None):
                for s in range(2):
                    pe.wait_ge(bank_read[2 + s], n_qkT(s) + 1)
                for t in range(NT):
                    if free:
                        free(t)
                    nc.tensor.matmul(ps_e[t][:], qkT[:, 0, t * P:(t + 1) * P], qkT[:, 1], start=True,
                                     stop=True).then_inc(scores_ready, 1)

            def turn_probs(b, last):
                pe.wait_ge(probs_done, NT * b + NT)
                for j in (2, 3, 0, 1):
                    pe.wait_ge(bank_read[j], n_probs(b, j, last))
                    for t in range(NT):
                        mm = nc.tensor.transpose(ps_t[j][:, t * P:(t + 1) * P], probs[:, t, j * P:(j + 1) * P], ident[:])
                    mm.then_inc(probsT_ready, 1)

            def turn_xn(b, last):
                pe.wait_ge(xn_done, NT * b + NT)
                for j in range(ND):
                    pe.wait_ge(bank_read[j], n_xn(b, j, last))
                    for t in range(NT):
                        mm = nc.tensor.transpose(ps_t[j][:, t * P:(t + 1) * P], xn[:, t, j * P:(j + 1) * P], ident[:])
                    mm.then_inc(xnT_ready, 1)

            def turn_x2n(b, n):
                pe.wait_ge(x2n_done, NT * b + NT)
                for j in range(ND):
                    pe.wait_ge(bank_read[j], n(j))
                    for t in range(NT):
                        mm = nc.tensor.transpose(ps_t[j][:, t * P:(t + 1) * P], x2n[:, t, j], ident[:])
                    mm.then_inc(x2T_ready, 1)

            def attend(b, last, free):
                for t in range(NT):
                    free(t)
                    for n, (u, v) in enumerate(((0, 0), (0, 1), (1, 0))):
                        for j in range(NT):
                            if t == 0 and n == 0:
                                if j == 0:
                                    pe.wait_ge(probsT_hi_done, NT * b + NT)
                                pe.wait_ge(xnT_hi_done, ND * b + j + 1)
                            if t == 0 and n == 1:
                                pe.wait_ge(bank_read[j], n_probs(b, j, last) + 1)
                            if t == 0 and n == 2:
                                pe.wait_ge(bank_read[j], n_xn(b, j, last) + 1)
                            mm = nc.tensor.matmul(ps_e[t][:], xnT[:, u, j, t * P:(t + 1) * P], probsT[:, v, j],
                                                  start=(n == 0 and j == 0), stop=(n == 2 and j == NT - 1))
                    mm.then_inc(attn_ready, 1)

            def step(b, first=False, last=False):
                if not last:
                    turn_ctx(b + 1, lambda k: pe.wait_ge(bank_read[k], n_ctx(b, k)))
                turn_probs(b, last)
                if not last:
                    project(lambda k: n_ctx(b, k), lambda s: pe.wait_ge(bank_read[2 + s], n_qk(b, s)))
                turn_xn(b, last)
                if not last:
                    scores(lambda s: n_qk(b, s), (lambda t: pe.wait_ge(exp_done, t + 1)) if first
                           else (lambda t: pe.wait_ge(x2_done, NT * b - NT + t + 1)))
                if not first:
                    turn_x2n(b - 1, lambda j: n_x2(b, j, last))
                attend(b, last, (lambda t: pe.wait_ge(x2_done, NT * b - NT + t + 1)) if last
                       else (lambda t: pe.wait_ge(exp_done, NT * b + NT + t + 1)))

            def hidden(b, g, x2T_here=None):
                for t in range(4):
                    pe.wait_ge(bank_read[t], n_hidden(b, g, t))
                    for v in range(2):
                        for j in range(ND):
                            if t == 0 and x2T_here:
                                x2T_here(v, j)
                            mm = nc.tensor.matmul(ps_t[t][:], w1T[:, g * 4 + t, j], x2T[:, v, b, j],
                                                  start=(v == 0 and j == 0), stop=(v == 1 and j == ND - 1))
                    mm.then_inc(hidden_ready, 1)

            def output(b, free):
                for t in range(NT):
                    free(t)
                    for k in range(NF):
                        if t == 0:
                            pe.wait_ge(bank_read[k % 4], n_hidden(b, k // 4, k % 4) + 1)
                        for part in (gT_hi, gT_lo):
                            mm = nc.tensor.matmul(ps_e[t][:], part[:, k, t * P:(t + 1) * P], w2T[:, k],
                                                  start=(k == 0 and part is gT_hi), stop=(k == NF - 1 and part is gT_lo))
                    mm.then_inc(y_ready, 1)

            pe.wait_ge(ident_done, 1)
            turn_ctx(0, lambda k: None)
            pe.wait_ge(small_in, 16 * 6)
            for s in range(2):
                for k in range(NC):
                    mm = nc.tensor.transpose(ps_t[2][:, (2 * s + k) * P:(2 * s + k + 1) * P],
                                             W_raw[:, s, k * P:(k + 1) * P], ident[:])
            mm.then_inc(WT_ready, 1)
            nc.tensor.transpose(ps_t[3][:, 0:NF], b1_rows[:], ident[0:NF, 0:NF]).then_inc(b1T_ready, 1)
            project(lambda k: 0, lambda s: pe.wait_ge(bank_read[2 + s], 1))
            scores(lambda s: 1)

            step(0, first=True)
            for b in range(1, LAST):
                step(b)
            step(LAST, last=True)

            pe.wait_ge(turned_done, NCH)
            with pe.Fori(0, GROUPS) as g:
                hidden(0, g)
            turn_x2n(LAST, lambda j: N_X2_LAST[j])
            pe.wait_ge(w2T_done, NF)
            output(0, lambda t: pe.wait_ge(x2_done, NT * LAST + t + 1))
            for j in range(ND):
                pe.wait_ge(bank_read[j], N_X2_LAST[j] + 1)
            with pe.Fori(1, B) as b:
                with pe.Fori(0, GROUPS) as g:
                    hidden(b, g)
                output(b, lambda t: pe.wait_ge(y_done, NT * b - NT + t + 1))

        @block.scalar
        def _(act):
            def copy_ctxT(b):
                for k in range(NC):
                    act.wait_ge(ctxT_ready, NC * b + k + 1)
                    nc.scalar.copy(ctxT[:, k], ps_t[k][:]).then_inc(bank_read[k], 1)

            def copy_qk(b):
                for s in range(2):
                    act.wait_ge(qk_ready, 2 * b + s + 1)
                    nc.scalar.activation(qkT[:, s], ps_t[2 + s][:], ACT.Identity,
                                         bias=bqk[:, s:s + 1]).then_inc(bank_read[2 + s], 1)

            def exps(b):
                for t in range(NT):
                    act.wait_ge(max_done, NT * b + t + 1)
                    nc.scalar.activation(probs[:, t], ps_e[t][:], ACT.Exp, bias=row_max[:, t:t + 1],
                                         accum_out=row_sum[:, t:t + 1]).then_inc(exp_done, 1)

            def high_probs(b):
                for n, j in enumerate((2, 3, 0, 1)):
                    act.wait_ge(probsT_ready, NT * b + n + 1)
                    nc.scalar.copy(probsT[:, 0, j], ps_t[j][:]).then_inc(probsT_hi_done, 1)

            def high_ln(ready, b, dst, done):
                for j in range(ND):
                    act.wait_ge(ready, ND * b + j + 1)
                    nc.scalar.mul(dst(j), ps_t[j][:], LN_SCALE).then_inc(done, 1)

            def sum_abs(m):
                flat = raws[m][:].rearrange("p a b -> p (a b)")
                for c in range(NCH):
                    if c % (NCH // 2) == 0:
                        act.wait_ge(w_here[m][c // (NCH // 2)], 16 * Q)
                    if m or c:
                        act.wait_ge(abs_done, NCH * m + c)
                    nc.scalar.activation(abs_out[:], flat[:, c * CH:(c + 1) * CH], ACT.Abs,
                                         accum_out=abs_sum[:, m, c:c + 1]).then_inc(abs_done, 1)

            def step(b, first=False, last=False):
                if not last:
                    copy_ctxT(b + 1)
                high_probs(b)
                if not last:
                    copy_qk(b + 1)
                high_ln(xnT_ready, b, lambda j: xnT[:, 0, j], xnT_hi_done)
                if not last:
                    exps(b + 1)
                if not first:
                    high_ln(x2T_ready, b - 1, lambda j: x2T[:, 0, b - 1, j], x2T_hi_done)

            def gelus(b, g):
                for pair in range(2):
                    for t in (2 * pair, 2 * pair + 1):
                        act.wait_ge(hidden_ready, NF * b + 4 * g + t + 1)
                        nc.scalar.activation(ps_t[t][:], ps_t[t][:], ACT.Gelu, scale=1.0 / LN_SCALE,
                                             bias=b1_col[:, bass.ds(4 * g + t, 1)]).then_inc(gelu_done, 1)
                    for t in (2 * pair, 2 * pair + 1):
                        act.wait_ge(gelu_done, NF * b + 4 * g + t + 1)
                        nc.scalar.activation(gT_hi[:, 4 * g + t], ps_t[t][:], ACT.Identity,
                                             scale=h_scale[:, bass.ds(4 * g + t, 1)]).then_inc(gT_hi_done, 1)

            act.wait_ge(ctx_here, 16)
            for m in range(2):
                n = raws[m].shape[1] // 2
                for h in range(2):
                    for q in range(Q):
                        act.dma_start(raws[m][q * R:(q + 1) * R, h * n:(h + 1) * n, :],
                                      w_views[m][q, :, h * n:(h + 1) * n, :]).then_inc(w_here[m][h], 16)

            copy_ctxT(0)
            act.wait_ge(WT_ready, 1)
            nc.scalar.copy(WT[:].rearrange("p s k h -> p (s k h)"), ps_t[2][:]).then_inc(bank_read[2], 1)
            act.wait_ge(small_in, 16 * 6)
            copy_qk(0)
            exps(0)
            step(0, first=True)
            sum_abs(0)
            for b in range(1, LAST):
                step(b)
            sum_abs(1)
            step(LAST, last=True)
            act.wait_ge(turned_done, NCH)
            act.wait_ge(h_scale_done, 1)
            with act.Fori(0, GROUPS) as g:
                gelus(0, g)
            high_ln(x2T_ready, LAST, lambda j: x2T[:, 0, LAST, j], x2T_hi_done)
            with act.Fori(1, B) as b:
                with act.Fori(0, GROUPS) as g:
                    gelus(b, g)

        @block.vector
        def _(dve):
            def low_probs(b):
                for n, j in enumerate((2, 3, 0, 1)):
                    dve.wait_ge(probsT_hi_done, NT * b + n + 1)
                    nc.vector.tensor_tensor(probsT[:, 1, j], ps_t[j][:], probsT[:, 0, j],
                                            ALU.subtract).then_inc(bank_read[j], 1)

            def low_ln(hi_done, b, hi, lo):
                for j in range(ND):
                    dve.wait_ge(hi_done, ND * b + j + 1)
                    nc.vector.scalar_tensor_tensor(out=lo(j), in0=ps_t[j][:], scalar=LN_SCALE, in1=hi(j),
                                                   op0=ALU.mult, op1=ALU.subtract).then_inc(bank_read[j], 1)

            def inverse(b, t):
                dve.wait_ge(exp_done, NT * b + t + 1)
                nc.vector.reciprocal(row_inv[:, t:t + 1], row_sum[:, t:t + 1]).then_inc(inv_done, 1)

            def maxima(b):
                for t in range(NT):
                    dve.wait_ge(scores_ready, NT * b + t + 1)
                    nc.vector.tensor_reduce(row_max[:, t:t + 1], ps_e[t][:], AX.X, ALU.max,
                                            negate=True).then_inc(max_done, 1)
                    if t >= 2:
                        inverse(b, t - 2)
                inverse(b, NT - 2)
                inverse(b, NT - 1)

            def moments(b, t, st, st_done, m, m_done):
                nc.vector.bn_stats(st[:, t], x_sb[:, b, t]).then_inc(st_done, 1)

            def aggregate(b, t, st, st_done, m, m_done):
                dve.wait_ge(st_done, NT * b + t + 1)
                nc.vector.bn_aggr(m[:, t], st[:, t]).then_inc(m_done, 1)

            def normalise(b):
                dve.wait_ge(x_here, 16 * b + 16)
                for t in range(NT):
                    moments(b, t, stats, stats_done, mv, mv_done)
                for t in range(NT):
                    aggregate(b, t, stats, stats_done, mv, mv_done)

            def apply_ln(b, first=False):
                dve.wait_ge(rstd_done, b + 1)
                if not first:
                    dve.wait_ge(xnT_ready, ND * b)
                for t in range(NT):
                    nc.vector.tensor_scalar(xn[:, t], x_sb[:, b, t], mv[:, t, 0:1], rstd[:, t:t + 1],
                                            ALU.subtract, ALU.mult).then_inc(xn_done, 1)

            def residual(b):
                for t in range(NT):
                    dve.wait_ge(attn_ready, NT * b + t + 1)
                    nc.vector.scalar_tensor_tensor(out=x_sb[:, b, t], in0=ps_e[t][:], scalar=1.0 / (LN_SCALE * PROB_SCALE),
                                                   in1=x_sb[:, b, t], op0=ALU.mult, op1=ALU.add).then_inc(x2_done, 1)
                    if t >= 1:
                        dve.wait_ge(x2_done, NT * b + t)
                        moments(b, t - 1, stats2, stats2_done, mv2, mv2_done)
                dve.wait_ge(x2_done, NT * b + NT)
                moments(b, NT - 1, stats2, stats2_done, mv2, mv2_done)
                for t in range(NT):
                    aggregate(b, t, stats2, stats2_done, mv2, mv2_done)

            def apply_ln2(b, first=False):
                dve.wait_ge(rstd2_done, b + 1)
                if first:
                    dve.wait_ge(WT_ready, 1)
                else:
                    dve.wait_ge(x2T_ready, ND * b)
                for t in range(NT):
                    nc.vector.tensor_scalar(x2n[:, t].rearrange("p j (q c) -> p q j c", q=Q),
                                            x_sb[:, b, t].rearrange("p (q j c) -> p q j c", q=Q, j=ND),
                                            mv2[:, t, 0:1], rstd2[:, t:t + 1],
                                            ALU.subtract, ALU.mult).then_inc(x2n_done, 1)

            def quantiser_cut(m):
                dve.wait_ge(abs_done, NCH * (m + 1))
                nc.vector.tensor_reduce(abs_row[:, m:m + 1], abs_sum[:, m], AX.X, ALU.add).then_inc(abs_row_done, 1)
                dve.wait_ge(abs_all_done, m + 1)
                nc.vector.tensor_scalar(cut[:, m, 0:1], abs_all[:, m:m + 1], 0.5 / (F * D), 0.5 * QUANT_EPS,
                                        ALU.mult, ALU.max).then_inc(cut_half, 1)
                dve.wait_ge(cut_half, m + 1)
                nc.vector.tensor_scalar(cut[:, m, 1:2], cut[:, m, 0:1], -1.0, None, ALU.mult).then_inc(cut_done, 1)
                dve.wait_ge(cut_done, m + 1)

            def quantise(m, c, done, dst):
                flat = raws[m][:].rearrange("p a b -> p (a b)")[:, bass.ds(c * CH, CH)]
                t_out = tern[:] if m == 0 else tern[:].bitcast(BF16)
                nc.vector.tensor_scalar(is_low[:], flat, cut[:, m, 1:2], None, ALU.is_lt).then_inc(is_low_done, 1)
                dve.wait_ge(is_low_done, done + 1)
                nc.vector.scalar_tensor_tensor(out=t_out, in0=flat, scalar=cut[:, m, 0:1], in1=is_low[:],
                                               op0=ALU.is_gt, op1=ALU.subtract).then_inc(tern_done, 1)
                dve.wait_ge(tern_done, done + 1)
                if m == 0:
                    src = t_out.rearrange("p (k j c) -> p k j c", j=ND, c=R)
                else:
                    src = t_out.rearrange("p (e k c) -> p e k c", k=NF, c=R)
                nc.vector.transpose(dst, src).then_inc(turned_done, 1)

            def quantise_w1(b):
                for i in range(NCH // 2):
                    c = (b - 1) * (NCH // 2) + i
                    q = (b - 1) * 2 + i // 2
                    k0 = NF // 2 * (i % 2)
                    quantise(0, c, c, w1T[:, k0:k0 + NF // 2, :, bass.ds(q * R, R)])

            def quantise_w2(c):
                n = D // NCH
                quantise(1, c, NCH + c, w2T[:, :, c * n:(c + 1) * n].rearrange("p k (e r) -> p e k r", r=R))

            def step(b, first=False, last=False):
                low_probs(b)
                low_ln(xnT_hi_done, b, lambda j: xnT[:, 0, j], lambda j: xnT[:, 1, j])
                if not last:
                    maxima(b + 1)
                if not first:
                    low_ln(x2T_hi_done, b - 1, lambda j: x2T[:, 0, b - 1, j], lambda j: x2T[:, 1, b - 1, j])
                if not last:
                    normalise(b + 1)
                    if not first:
                        quantise_w1(b)
                    apply_ln(b + 1)
                residual(b)
                apply_ln2(b, first)

            def low_gelus(b, g):
                for t in range(4):
                    dve.wait_ge(gT_hi_done, NF * b + 4 * g + t + 1)
                    nc.vector.scalar_tensor_tensor(out=gT_lo[:, 4 * g + t], in0=ps_t[t][:],
                                                   scalar=h_scale[:, bass.ds(4 * g + t, 1)], in1=gT_hi[:, 4 * g + t],
                                                   op0=ALU.mult, op1=ALU.subtract).then_inc(bank_read[t], 1)

            def results(b):
                for t in range(NT):
                    dve.wait_ge(y_ready, NT * b + t + 1)
                    dve.wait_ge(b2_added, NT * b + t + 1)
                    nc.vector.tensor_tensor(x_sb[:, b, t], ps_e[t][:], x_sb[:, b, t], ALU.add).then_inc(y_done, 1)

            nc.vector.memset(minus_half[:], -0.5).then_inc(minus_half_done, 1)
            normalise(0)
            dve.wait_ge(b1T_ready, 1)
            nc.vector.tensor_copy(b1_col[:], ps_t[3][:, 0:NF]).then_inc(bank_read[3], 1)
            dve.wait_ge(bank_read[3], 1)
            nc.vector.tensor_scalar(bound[:].bitcast(I32), b1_col[:].bitcast(I32), 0x7FFFFFFF, None,
                                    ALU.bitwise_and).then_inc(bound_step, 1)
            dve.wait_ge(bound_step, 1)
            nc.vector.tensor_scalar(bound[:], bound[:], float(D + 1), None, ALU.add).then_inc(bound_step, 1)
            dve.wait_ge(bound_step, 2)
            nc.vector.tensor_scalar(bound[:].bitcast(I32), bound[:].bitcast(I32), 0x7F800000, None,
                                    ALU.bitwise_and).then_inc(bound_step, 1)
            dve.wait_ge(bound_step, 3)
            nc.vector.tensor_scalar(h_unscale[:], bound[:], 1.0 / HIDDEN_TOP, None, ALU.mult).then_inc(bound_step, 1)
            dve.wait_ge(bound_step, 4)
            nc.vector.reciprocal(h_scale[:], h_unscale[:]).then_inc(h_scale_done, 1)
            apply_ln(0, first=True)
            maxima(0)
            step(0, first=True)
            quantiser_cut(0)
            for b in range(1, LAST):
                step(b)
            quantiser_cut(1)
            step(LAST, last=True)
            dve.wait_ge(turned_done, NCH)
            for c in range(NCH):
                quantise_w2(c)
            dve.wait_ge(turned_done, 2 * NCH)
            for k in range(NF):
                nc.vector.tensor_scalar(w2T[:, k], w2T[:, k], h_unscale[:, k:k + 1], None, ALU.mult).then_inc(w2T_done, 1)
            with dve.Fori(0, GROUPS) as g:
                low_gelus(0, g)
            low_ln(x2T_hi_done, LAST, lambda j: x2T[:, 0, LAST, j], lambda j: x2T[:, 1, LAST, j])
            results(0)
            with dve.Fori(1, B) as b:
                with dve.Fori(0, GROUPS) as g:
                    low_gelus(b, g)
                results(b)


_INS = ["x", "ctx_1024", "L0_xattn_Wq", "L0_xattn_bq", "L0_xattn_Wk", "L0_xattn_bk",
        "L0_ffn_w1", "L0_ffn_b1", "L0_ffn_w2", "L0_ffn_b2"]


def kernel(**inputs):
    import numpy as np
    import concourse.bacc as bacc
    from concourse.bass_utils import run_bass_kernel_spmd

    nc = bacc.Bacc("TRN2", target_bir_lowering=False, num_devices=1)
    arrays, args = {}, []
    for name in _INS:
        a = np.ascontiguousarray(inputs[name])
        arrays[f"in_{name}"] = a
        args.append(nc.dram_tensor(f"in_{name}", a.shape, mybir.dt.from_np(a.dtype), kind="ExternalInput").ap())
    shape = arrays["in_x"].shape
    out = nc.dram_tensor("out", shape, F32, kind="ExternalOutput").ap()
    xattn_ffn(nc, *args, out)
    r = run_bass_kernel_spmd(nc, [arrays], core_ids=[0])
    return r.results[0]["out"]
```

```python
from contextlib import ExitStack

import concourse.bass as bass
from concourse import mybir
from concourse.alu_op_type import AluOpType as ALU

ACT = mybir.ActivationFunctionType
AX = mybir.AxisListType
F32 = mybir.dt.float32
F16 = mybir.dt.float16
BF16 = mybir.dt.bfloat16
U8 = mybir.dt.uint8
I32 = mybir.dt.int32

LN_SCALE = 2.0 ** 10
PROB_SCALE = 2.0 ** 15
HIDDEN_TOP = 2.0 ** 14
LN_EPS = 1e-5
QUANT_EPS = 1e-8
ROUND = 1.5 * 2.0 ** 23


def xattn_ffn(nc, x, ctx_in, Wq, bq, Wk, bk, w1, b1, w2, b2, out):
    B, L, D = x.shape
    C = ctx_in.shape[2]
    H = Wq.shape[0]
    F = w1.shape[0]
    P = 128
    NT = L // P
    NC = C // P
    ND = D // P
    NF = F // P
    Q = 4
    R = P // Q
    NCH = 8
    WN = F * D // P
    CH = WN // NCH
    assert ctx_in.shape[1] == L and D == L and H == P and D == ND * P

    with ExitStack() as stack:
        def sb(name, shape, dt=F32):
            return stack.enter_context(nc.sbuf_tensor(name, shape, dt))

        def sem(name):
            return stack.enter_context(nc.semaphore(name))

        x_sb = sb("x_sb", [P, B, NT, D])
        w1_raw = sb("w1_raw", [P, F // R, P])
        w2_raw = sb("w2_raw", [P, D // R, F // Q])
        w1T = sb("w1T", [P, NF, ND, P], F16)
        x2T = sb("x2T", [P, 2, B, ND, L], F16)
        scratch = sb("scratch", [P, 2, NT, D])
        probs = scratch[:, 0]
        xn = scratch[:, 1]
        x2n = sb("x2n", [P, NT, ND, P])
        W_raw = x2n[:, 0:2].rearrange("p a b c -> p a (b c)")[:, :, 0:C]
        ctx_sb = sb("ctx_sb", [P, NT, C])
        ctxT = sb("ctxT", [P, NC, L])
        qkT = sb("qkT", [P, 2, L])
        WT = sb("WT", [P, 2, NC, H])
        xnT = sb("xnT", [P, 2, ND, L], F16)
        probsT = sb("probsT", [P, 2, NT, L], F16)
        whole = sb("whole", [P, CH], F16)
        tern = sb("tern", [P, CH], F16)
        abs_out = sb("abs_out", [P, CH], U8)
        x_out = sb("x_out", [P, D], U8)
        b2_sb = sb("b2_sb", [P, D])
        ident = sb("ident", [P, P])
        b1_rows = sb("b1_rows", [NF, P])
        b1_col = sb("b1_col", [P, NF])
        bqk = sb("bqk", [P, 2])
        h_scale = sb("h_scale", [P, NF])
        h_unscale = sb("h_unscale", [P, NF])
        bound = sb("bound", [P, NF])
        abs_sum = sb("abs_sum", [P, 2, NCH])
        abs_row = sb("abs_row", [P, 2])
        abs_all = sb("abs_all", [P, 2])
        scale = sb("scale", [P, 2])
        inv_scale = sb("inv_scale", [P, 2])
        stats = sb("stats", [P, NT, 6])
        mv = sb("mv", [P, NT, 2])
        var_eps = sb("var_eps", [P, NT])
        neg_mean = sb("neg_mean", [P, NT])
        xsum = sb("xsum", [P, NT])
        xsquare = sb("xsquare", [P, NT])
        rstd = sb("rstd", [P, NT])
        stats2 = sb("stats2", [P, NT, 6])
        mv2 = sb("mv2", [P, NT, 2])
        var_eps2 = sb("var_eps2", [P, NT])
        neg_mean2 = sb("neg_mean2", [P, NT])
        rstd2 = sb("rstd2", [P, NT])
        minus_half = sb("minus_half", [P, NT])
        row_max = sb("row_max", [P, NT])
        row_sum = sb("row_sum", [P, NT])
        row_inv = sb("row_inv", [P, NT])

        w1_flat = w1_raw[:].rearrange("p a b -> p (a b)")
        w2T = w1_flat[:, 0:WN // 2].bitcast(BF16).rearrange("p (k e) -> p k e", k=NF)
        gT_hi = w1_flat[:, WN // 2:WN].bitcast(F16).rearrange("p (k t) -> p k t", k=NF)
        gT_lo = scratch[:].rearrange("p a b c -> p (a b c)").bitcast(F16).rearrange("p (k t) -> p k t", k=NF)

        ps_t = [stack.enter_context(nc.psum_tensor(f"ps_t{i}", [P, L], F32)) for i in range(4)]
        ps_e = [stack.enter_context(nc.psum_tensor(f"ps_e{i}", [P, L], F32)) for i in range(4)]

        W_here, small_in = sem("W_here"), sem("small_in")
        ctx_here = sem("ctx_here")
        x_here = sem("x_here")
        w_here = [[sem(f"w{m + 1}_here{h}") for h in range(2)] for m in range(2)]
        b2_here, out_done = sem("b2_here"), sem("out_done")
        ident_zero, ident_done = sem("ident_zero"), sem("ident_done")
        neg_mean_done = sem("neg_mean_done")
        ln_step, rstd_done, xn_done = sem("ln_step"), sem("rstd_done"), sem("xn_done")
        ln2_step, rstd2_done, x2n_done = sem("ln2_step"), sem("rstd2_done"), sem("x2n_done")
        rounded = sem("rounded")
        probs_done = sem("probs_done")
        b2_added = sem("b2_added")
        abs_all_done = sem("abs_all_done")
        WT_ready, b1T_ready = sem("WT_ready"), sem("b1T_ready")
        ctxT_ready, qk_ready, scores_ready = sem("ctxT_ready"), sem("qk_ready"), sem("scores_ready")
        xnT_ready, probsT_ready, attn_ready = sem("xnT_ready"), sem("probsT_ready"), sem("attn_ready")
        x2T_ready, hidden_ready, y_ready = sem("x2T_ready"), sem("hidden_ready"), sem("y_ready")
        exp_done, abs_done = sem("exp_done"), sem("abs_done")
        xsum_done, xsquare_done = sem("xsum_done"), sem("xsquare_done")
        probsT_hi_done, xnT_hi_done, x2T_hi_done = sem("probsT_hi_done"), sem("xnT_hi_done"), sem("x2T_hi_done")
        gelu_done, gT_hi_done = sem("gelu_done"), sem("gT_hi_done")
        stats_done, mv_done = sem("stats_done"), sem("mv_done")
        stats2_done, mv2_done = sem("stats2_done"), sem("mv2_done")
        max_done, inv_done, x2_done, y_done = sem("max_done"), sem("inv_done"), sem("x2_done"), sem("y_done")
        abs_row_done, scale_done, inv_scale_done = sem("abs_row_done"), sem("scale_done"), sem("inv_scale_done")
        whole_done, tern_done, turned_done = sem("whole_done"), sem("tern_done"), sem("turned_done")
        bound_step, h_scale_done, w2T_done = sem("bound_step"), sem("h_scale_done"), sem("w2T_done")
        minus_half_done = sem("minus_half_done")
        bank_read = [sem(f"bank_read{j}") for j in range(4)]

        LAST = B - 1

        def before_step(b, j):
            if b == 0:
                return 1 if j < 2 else 2
            return 4 * b + (0 if j < 2 else 1)

        def n_ctx(b, j):
            return before_step(b, j)

        def n_xn(b, j):
            return before_step(b, j) + (1 if j < 2 and b < LAST else 0)

        def n_qk(b, s):
            return before_step(b, 2 + s) + 1

        def n_probs(b, j):
            return before_step(b, j) + (2 if b < LAST else 1)

        def n_x2(b, j):
            return before_step(b, j) + (3 if b < LAST else 2)

        BY_ACT = 2

        W1_PLAN = [[[], [], [], [], []], [[], [], [0], [1], []], [[], [2], [3], [4], []], [[], [5], [6], [7], []]]

        def chunk_views(m, c):
            if m == 0:
                src = w1_raw[:].rearrange("p (q k) e -> p q k e", q=Q)[:, :, 2 * c:2 * c + 2]
                dst = w1T[:, 2 * c:2 * c + 2].rearrange("p k j (q r) -> p q (k j) r", q=Q)
            else:
                src = w2_raw[:].rearrange("p e (k c) -> p e k c", c=R)[:, :, 2 * c:2 * c + 2]
                dst = w2T[:, 2 * c:2 * c + 2].rearrange("p k (e r) -> p e k r", r=R)
            return src, dst

        def chunk_shape(m, flat):
            if m == 0:
                return flat.rearrange("p (q k e) -> p q k e", q=Q, k=2)
            return flat.rearrange("p (e k c) -> p e k c", k=2, c=R)

        XN_ORDER = (2, 3, 0, 1)

        AFTER_A = [before_step(LAST, j) + 3 for j in range(4)]
        GROUPS = NF // 4

        def n_hidden(b, g, j):
            first = isinstance(b, int) and b == 0
            return AFTER_A[j] + g if first else AFTER_A[j] + GROUPS * b + 1 + g

        N_X2_LAST = [AFTER_A[j] + GROUPS for j in range(4)]

        x_tiles = x.rearrange("b (t p) d -> b p t d", p=P)
        ctx_tiles = ctx_in.rearrange("b (t p) c -> b p t c", p=P)
        out_tiles = out.rearrange("b (t p) d -> b p t d", p=P)
        w_views = [w1.rearrange("(fb r) (q d) -> q r fb d", r=R, q=Q), w2.rearrange("(eb r) (q f) -> q r eb f", r=R, q=Q)]
        b1_view = b1.rearrange("(q k c) -> k q c", q=Q, k=NF)
        raws = [w1_raw, w2_raw]

        block = stack.enter_context(nc.Block())

        @block.sync
        def _(sp):
            def load_ctx(b):
                if b:
                    sp.wait_ge(ctxT_ready, NC * b)
                sp.dma_start(ctx_sb[:], ctx_tiles[b]).then_inc(ctx_here, 16)

            def load_x(b):
                if b:
                    sp.wait_ge(x_here, 16 * b)
                sp.dma_start(x_sb[:, b], x_tiles[b]).then_inc(x_here, 16)

            def load_w(m, h):
                n = raws[m].shape[1] // 2
                for q in range(Q):
                    sp.dma_start(raws[m][q * R:(q + 1) * R, h * n:(h + 1) * n, :],
                                 w_views[m][q, :, h * n:(h + 1) * n, :]).then_inc(w_here[m][h], 16)

            load_ctx(0)
            sp.dma_start(W_raw[:, 0, :], Wq).then_inc(W_here, 16)
            sp.dma_start(W_raw[:, 1, :], Wk).then_inc(W_here, 16)
            sp.dma_start(b1_rows[:].rearrange("k (q c) -> k q c", q=Q), b1_view).then_inc(small_in, 16)
            load_x(0)
            sp.dma_start(bqk[:, 0:1], bq.rearrange("(p a) -> p a", a=1)).then_inc(small_in, 16)
            sp.dma_start(bqk[:, 1:2], bk.rearrange("(p a) -> p a", a=1)).then_inc(small_in, 16)
            load_w(0, 0)
            load_ctx(1)
            load_x(1)
            load_w(0, 1)
            sp.dma_start(b2_sb[:], b2.rearrange("(a d) -> a d", a=1).to_broadcast([P, D])).then_inc(b2_here, 16)
            load_w(1, 0)
            load_ctx(2)
            load_x(2)
            load_w(1, 1)
            load_ctx(3)
            load_x(3)
            with sp.Fori(0, B) as b:
                for t in range(NT):
                    sp.wait_ge(y_done, NT * b + t + 1)
                    sp.dma_start(out_tiles[b, :, t], x_sb[:, b, t]).then_inc(out_done, 16)
            sp.wait_ge(out_done, 16 * B * NT)

        @block.gpsimd
        def _(pool):
            def inverse_std(b, mv_t, ready, ve, nm, step_done, r, r_done):
                pool.wait_ge(ready, NT * b + NT)
                nc.gpsimd.tensor_scalar(ve[:], mv_t[:, :, 1], LN_EPS, None, ALU.add).then_inc(step_done, 1)
                nc.gpsimd.tensor_scalar(nm[:], mv_t[:, :, 0], -1.0, None, ALU.mult).then_inc(step_done, 1)
                pool.wait_ge(step_done, 2 * b + 2)
                nc.gpsimd.tensor_tensor(r[:], ve[:], minus_half[:], ALU.pow).then_inc(r_done, 1)
                pool.wait_ge(r_done, b + 1)

            def mean_of_sums(b):
                pool.wait_ge(xsum_done, NT * (b - BY_ACT + 1))
                nc.gpsimd.tensor_scalar(neg_mean[:], xsum[:], -1.0 / D, 1.0, ALU.mult, ALU.mult).then_inc(neg_mean_done, 1)

            def inverse_std_of_sums(b):
                n = b - BY_ACT
                pool.wait_ge(xsquare_done, NT * (n + 1))
                nc.gpsimd.tensor_scalar(var_eps[:], xsquare[:], 1.0 / D, LN_EPS, ALU.mult, ALU.add).then_inc(ln_step, 1)
                pool.wait_ge(ln_step, 2 * BY_ACT + n + 1)
                nc.gpsimd.tensor_tensor(rstd[:], var_eps[:], minus_half[:], ALU.pow).then_inc(rstd_done, 1)
                pool.wait_ge(rstd_done, b + 1)

            def layernorm(b):
                if b < BY_ACT:
                    inverse_std(b, mv, mv_done, var_eps, neg_mean, ln_step, rstd, rstd_done)
                else:
                    inverse_std_of_sums(b)
                if b:
                    pool.wait_ge(xnT_ready, ND * b)
                for t in range(NT):
                    nc.gpsimd.tensor_scalar(xn[:, t], x_sb[:, b, t], neg_mean[:, t:t + 1], rstd[:, t:t + 1],
                                            ALU.add, ALU.mult).then_inc(xn_done, 1)

            def layernorm2(b):
                inverse_std(b, mv2, mv2_done, var_eps2, neg_mean2, ln2_step, rstd2, rstd2_done)
                if b:
                    pool.wait_ge(x2T_ready, ND * b)
                else:
                    pool.wait_ge(WT_ready, 1)
                for t in range(NT):
                    nc.gpsimd.tensor_scalar(x2n[:, t].rearrange("p j (q c) -> p q j c", q=Q),
                                            x_sb[:, b, t].rearrange("p (q j c) -> p q j c", q=Q, j=ND),
                                            neg_mean2[:, t:t + 1], rstd2[:, t:t + 1],
                                            ALU.add, ALU.mult).then_inc(x2n_done, 1)

            def normalise_probs(b):
                for t in range(NT):
                    pool.wait_ge(inv_done, NT * b + t + 1)
                    nc.gpsimd.tensor_scalar(probs[:, t], probs[:, t], row_inv[:, t:t + 1], PROB_SCALE,
                                            ALU.mult, ALU.mult).then_inc(probs_done, 1)

            def add_b2(b):
                if b == 0:
                    pool.wait_ge(b2_here, 16)
                for t in range(NT):
                    pool.wait_ge(x2n_done, NT * b + t + 1)
                    nc.gpsimd.tensor_tensor(x_sb[:, b, t], x_sb[:, b, t], b2_sb[:], ALU.add).then_inc(b2_added, 1)

            def weight_total(m):
                pool.wait_ge(abs_row_done, m + 1)
                nc.gpsimd.partition_all_reduce(abs_all[:, m:m + 1], abs_row[:, m:m + 1], P,
                                               bass.bass_isa.ReduceOp.add).then_inc(abs_all_done, 1)

            def round_weights(m, chunks):
                pool.wait_ge(inv_scale_done, m + 1)
                for c in chunks:
                    src, _ = chunk_views(m, c)
                    nc.gpsimd.tensor_scalar(src, src, inv_scale[:, m:m + 1], ROUND, ALU.mult,
                                            ALU.add).then_inc(rounded, 1)

            def unscale(c):
                pool.wait_ge(turned_done, NCH + c + 1)
                for k in (2 * c, 2 * c + 1):
                    nc.gpsimd.tensor_scalar(w2T[:, k], w2T[:, k], h_unscale[:, k:k + 1], 1.0,
                                            ALU.mult, ALU.mult).then_inc(w2T_done, 1)

            nc.gpsimd.memset(ident[:], 0.0).then_inc(ident_zero, 1)
            pool.wait_ge(ident_zero, 1)
            nc.gpsimd.affine_select(out=ident[:], in_=ident[:], compare_op=ALU.not_equal, fill=1.0, base=0,
                                    pattern=[[-1, P]], channel_multiplier=1).then_inc(ident_done, 1)
            pool.wait_ge(minus_half_done, 1)
            layernorm(0)
            normalise_probs(0)
            for b in range(B):
                if BY_ACT <= b + 1 < B:
                    mean_of_sums(b + 1)
                if b < LAST:
                    normalise_probs(b + 1)
                    layernorm(b + 1)
                else:
                    add_b2(0)
                    round_weights(1, range(NCH))
                layernorm2(b)
                if b == 0 or b == 2:
                    weight_total(b // 2)
                if b == 0:
                    round_weights(0, (0, 1))
                elif b == 1:
                    round_weights(0, (2, 3, 4))
                elif b == 2:
                    round_weights(0, (5, 6, 7))
            for c in range(NCH):
                unscale(c)
            for b in range(1, B):
                add_b2(b)

        @block.tensor
        def _(pe):
            def turn_ctx(b, n):
                pe.wait_ge(ctx_here, 16 * b + 16)
                for k in range(NC):
                    n(k)
                    for t in range(NT):
                        mm = nc.tensor.transpose(ps_t[k][:, t * P:(t + 1) * P], ctx_sb[:, t, k * P:(k + 1) * P], ident[:])
                    mm.then_inc(ctxT_ready, 1)

            def project(n_ctxT, n):
                for s in range(2):
                    n(s)
                    for k in range(NC):
                        if s == 0:
                            pe.wait_ge(bank_read[k], n_ctxT(k) + 1)
                        mm = nc.tensor.matmul(ps_t[2 + s][:], WT[:, s, k], ctxT[:, k], start=(k == 0), stop=(k == NC - 1))
                    mm.then_inc(qk_ready, 1)

            def scores(n_qkT, free=None):
                for s in range(2):
                    pe.wait_ge(bank_read[2 + s], n_qkT(s) + 1)
                for t in range(NT):
                    if free:
                        free(t)
                    nc.tensor.matmul(ps_e[t][:], qkT[:, 0, t * P:(t + 1) * P], qkT[:, 1], start=True,
                                     stop=True).then_inc(scores_ready, 1)

            def turn_probs(b):
                pe.wait_ge(probs_done, NT * b + NT)
                for j in range(NT):
                    pe.wait_ge(bank_read[j], n_probs(b, j))
                    for t in range(NT):
                        mm = nc.tensor.transpose(ps_t[j][:, t * P:(t + 1) * P], probs[:, t, j * P:(j + 1) * P], ident[:])
                    mm.then_inc(probsT_ready, 1)

            def turn_xn(b):
                pe.wait_ge(xn_done, NT * b + NT)
                for j in XN_ORDER:
                    pe.wait_ge(bank_read[j], n_xn(b, j))
                    for t in range(NT):
                        mm = nc.tensor.transpose(ps_t[j][:, t * P:(t + 1) * P], xn[:, t, j * P:(j + 1) * P], ident[:])
                    mm.then_inc(xnT_ready, 1)

            def turn_x2n(b, n):
                pe.wait_ge(x2n_done, NT * b + NT)
                for j in range(ND):
                    pe.wait_ge(bank_read[j], n(j))
                    for t in range(NT):
                        mm = nc.tensor.transpose(ps_t[j][:, t * P:(t + 1) * P], x2n[:, t, j], ident[:])
                    mm.then_inc(x2T_ready, 1)

            def attend(b, free):
                for t in range(NT):
                    free(t)
                    for n, (u, v) in enumerate(((0, 0), (0, 1), (1, 0))):
                        for j in range(NT):
                            if t == 0 and n == 0:
                                if j == 0:
                                    pe.wait_ge(xnT_hi_done, ND * b + ND)
                                pe.wait_ge(probsT_hi_done, NT * b + j + 1)
                            if t == 0 and n == 1:
                                pe.wait_ge(bank_read[j], n_probs(b, j) + 1)
                            if t == 0 and n == 2:
                                pe.wait_ge(bank_read[j], n_xn(b, j) + 1)
                            mm = nc.tensor.matmul(ps_e[t][:], xnT[:, u, j, t * P:(t + 1) * P], probsT[:, v, j],
                                                  start=(n == 0 and j == 0), stop=(n == 2 and j == NT - 1))
                    mm.then_inc(attn_ready, 1)

            def step(b):
                if b < LAST:
                    turn_ctx(b + 1, lambda k: pe.wait_ge(bank_read[k], n_ctx(b, k)))
                turn_xn(b)
                if b < LAST:
                    project(lambda k: n_ctx(b, k), lambda s: pe.wait_ge(bank_read[2 + s], n_qk(b, s)))
                turn_probs(b)

                def e_bank_taken_to_sbuf(t):
                    if b:
                        pe.wait_ge(x2_done, NT * b - NT + t + 1)
                    else:
                        pe.wait_ge(exp_done, t + 1)

                if b < LAST:
                    scores(lambda s: n_qk(b, s), e_bank_taken_to_sbuf)
                if b > 0:
                    turn_x2n(b - 1, lambda j: n_x2(b, j))
                if b < LAST:
                    attend(b, lambda t: pe.wait_ge(exp_done, NT * b + NT + t + 1))
                else:
                    attend(b, e_bank_taken_to_sbuf)

            def hidden(b, g, first_weights=False):
                for t in range(4):
                    if first_weights and t % 2 == 0:
                        pe.wait_ge(turned_done, 2 * g + t // 2 + 1)
                    pe.wait_ge(bank_read[t], n_hidden(b, g, t))
                    for v in range(2):
                        for j in range(ND):
                            mm = nc.tensor.matmul(ps_t[t][:], w1T[:, g * 4 + t, j], x2T[:, v, b, j],
                                                  start=(v == 0 and j == 0), stop=(v == 1 and j == ND - 1))
                    mm.then_inc(hidden_ready, 1)

            def output(b, free, first_weights=False):
                for t in range(NT):
                    free(t)
                    for k in range(NF):
                        if t == 0 and first_weights:
                            pe.wait_ge(w2T_done, k + 1)
                        if t == 0:
                            pe.wait_ge(bank_read[k % 4], n_hidden(b, k // 4, k % 4) + 1)
                        for part in (gT_hi, gT_lo):
                            mm = nc.tensor.matmul(ps_e[t][:], part[:, k, t * P:(t + 1) * P], w2T[:, k],
                                                  start=(k == 0 and part is gT_hi), stop=(k == NF - 1 and part is gT_lo))
                    mm.then_inc(y_ready, 1)

            pe.wait_ge(ident_done, 1)
            turn_ctx(0, lambda k: None)
            pe.wait_ge(W_here, 16 * 2)
            for s in range(2):
                for k in range(NC):
                    mm = nc.tensor.transpose(ps_t[2][:, (2 * s + k) * P:(2 * s + k + 1) * P],
                                             W_raw[:, s, k * P:(k + 1) * P], ident[:])
            mm.then_inc(WT_ready, 1)
            pe.wait_ge(small_in, 16 * 3)
            nc.tensor.transpose(ps_t[3][:, 0:NF], b1_rows[:], ident[0:NF, 0:NF]).then_inc(b1T_ready, 1)
            project(lambda k: 0, lambda s: pe.wait_ge(bank_read[2 + s], 1))
            scores(lambda s: 1)

            for b in range(B):
                step(b)

            with pe.Fori(0, GROUPS) as g:
                hidden(0, g, first_weights=True)
            output(0, lambda t: pe.wait_ge(x2_done, NT * LAST + t + 1), first_weights=True)
            turn_x2n(LAST, lambda j: N_X2_LAST[j])
            with pe.Fori(1, B) as b:
                with pe.Fori(0, GROUPS) as g:
                    hidden(b, g)
                output(b, lambda t: pe.wait_ge(y_done, NT * b - NT + t + 1))

        @block.scalar
        def _(act):
            def copy_ctxT(b):
                for k in range(NC):
                    act.wait_ge(ctxT_ready, NC * b + k + 1)
                    nc.scalar.copy(ctxT[:, k], ps_t[k][:]).then_inc(bank_read[k], 1)

            def copy_qk(b):
                for s in range(2):
                    act.wait_ge(qk_ready, 2 * b + s + 1)
                    nc.scalar.activation(qkT[:, s], ps_t[2 + s][:], ACT.Identity,
                                         bias=bqk[:, s:s + 1]).then_inc(bank_read[2 + s], 1)

            def exps(b):
                for t in range(NT):
                    act.wait_ge(max_done, NT * b + t + 1)
                    nc.scalar.activation(probs[:, t], ps_e[t][:], ACT.Exp, bias=row_max[:, t:t + 1],
                                         accum_out=row_sum[:, t:t + 1]).then_inc(exp_done, 1)

            def high_probs(b):
                for n, j in enumerate(range(NT)):
                    act.wait_ge(probsT_ready, NT * b + n + 1)
                    nc.scalar.copy(probsT[:, 0, j], ps_t[j][:]).then_inc(probsT_hi_done, 1)

            def high_ln(ready, b, order, dst, done):
                for n, j in enumerate(order):
                    act.wait_ge(ready, ND * b + n + 1)
                    nc.scalar.mul(dst(j), ps_t[j][:], LN_SCALE).then_inc(done, 1)

            def sum_x(b):
                act.wait_ge(x_here, 16 * b + 16)
                if b > BY_ACT:
                    act.wait_ge(xsquare_done, NT * (b - BY_ACT))
                for t in range(NT):
                    if t:
                        act.wait_ge(xsum_done, NT * (b - BY_ACT) + t)
                    nc.scalar.activation(x_out[:], x_sb[:, b, t], ACT.Identity,
                                         accum_out=xsum[:, t:t + 1]).then_inc(xsum_done, 1)

            def sum_squares(b):
                act.wait_ge(neg_mean_done, b - BY_ACT + 1)
                for t in range(NT):
                    if t:
                        act.wait_ge(xsquare_done, NT * (b - BY_ACT) + t)
                    nc.scalar.activation(x_out[:], x_sb[:, b, t], ACT.Square, bias=neg_mean[:, t:t + 1],
                                         accum_out=xsquare[:, t:t + 1]).then_inc(xsquare_done, 1)

            def sum_abs(m, chunks=range(NCH)):
                flat = raws[m][:].rearrange("p a b -> p (a b)")
                for c in chunks:
                    if c % (NCH // 2) == 0:
                        act.wait_ge(w_here[m][c // (NCH // 2)], 16 * Q)
                    if m or c:
                        act.wait_ge(abs_done, NCH * m + c)
                    nc.scalar.activation(abs_out[:], flat[:, c * CH:(c + 1) * CH], ACT.Abs,
                                         accum_out=abs_sum[:, m, c:c + 1]).then_inc(abs_done, 1)

            def step(b):
                if b < LAST:
                    copy_ctxT(b + 1)
                high_ln(xnT_ready, b, XN_ORDER, lambda j: xnT[:, 0, j], xnT_hi_done)
                if BY_ACT <= b + 1 < B:
                    sum_x(b + 1)
                if b < LAST:
                    copy_qk(b + 1)
                high_probs(b)
                if b < LAST:
                    exps(b + 1)
                if b > 0:
                    high_ln(x2T_ready, b - 1, range(ND), lambda j: x2T[:, 0, b - 1, j], x2T_hi_done)
                if BY_ACT <= b + 1 < B:
                    sum_squares(b + 1)
                if b == 0:
                    sum_abs(0)
                elif b < LAST:
                    sum_abs(1, range((b - 1) * NCH // 2, b * NCH // 2))

            def gelus(b, g):
                for pair in range(2):
                    for t in (2 * pair, 2 * pair + 1):
                        act.wait_ge(hidden_ready, NF * b + 4 * g + t + 1)
                        nc.scalar.activation(ps_t[t][:], ps_t[t][:], ACT.Gelu, scale=1.0 / LN_SCALE,
                                             bias=b1_col[:, bass.ds(4 * g + t, 1)]).then_inc(gelu_done, 1)
                    for t in (2 * pair, 2 * pair + 1):
                        act.wait_ge(gelu_done, NF * b + 4 * g + t + 1)
                        nc.scalar.activation(gT_hi[:, 4 * g + t], ps_t[t][:], ACT.Identity,
                                             scale=h_scale[:, bass.ds(4 * g + t, 1)]).then_inc(gT_hi_done, 1)

            copy_ctxT(0)
            act.wait_ge(WT_ready, 1)
            nc.scalar.copy(WT[:].rearrange("p s k h -> p (s k h)"), ps_t[2][:]).then_inc(bank_read[2], 1)
            act.wait_ge(small_in, 16 * 3)
            copy_qk(0)
            exps(0)
            for b in range(B):
                step(b)
            act.wait_ge(turned_done, NCH)
            act.wait_ge(h_scale_done, 1)
            gelus(0, 0)
            with act.Fori(1, GROUPS) as g:
                gelus(0, g)
            high_ln(x2T_ready, LAST, range(ND), lambda j: x2T[:, 0, LAST, j], x2T_hi_done)
            with act.Fori(1, B) as b:
                with act.Fori(0, GROUPS) as g:
                    gelus(b, g)

        @block.vector
        def _(dve):
            def low_probs(b):
                for n, j in enumerate(range(NT)):
                    dve.wait_ge(probsT_hi_done, NT * b + n + 1)
                    nc.vector.tensor_tensor(probsT[:, 1, j], ps_t[j][:], probsT[:, 0, j],
                                            ALU.subtract).then_inc(bank_read[j], 1)

            def low_ln(hi_done, b, order, hi, lo):
                for n, j in enumerate(order):
                    dve.wait_ge(hi_done, ND * b + n + 1)
                    nc.vector.scalar_tensor_tensor(out=lo(j), in0=ps_t[j][:], scalar=LN_SCALE, in1=hi(j),
                                                   op0=ALU.mult, op1=ALU.subtract).then_inc(bank_read[j], 1)

            def inverse(b, t):
                dve.wait_ge(exp_done, NT * b + t + 1)
                nc.vector.reciprocal(row_inv[:, t:t + 1], row_sum[:, t:t + 1]).then_inc(inv_done, 1)

            def maxima(b):
                for t in range(NT):
                    dve.wait_ge(scores_ready, NT * b + t + 1)
                    nc.vector.tensor_reduce(row_max[:, t:t + 1], ps_e[t][:], AX.X, ALU.max,
                                            negate=True).then_inc(max_done, 1)
                    if t >= 2:
                        inverse(b, t - 2)

            def moments(b):
                dve.wait_ge(x_here, 16 * b + 16)
                for t in range(NT):
                    nc.vector.bn_stats(stats[:, t], x_sb[:, b, t]).then_inc(stats_done, 1)
                for t in range(NT):
                    dve.wait_ge(stats_done, NT * b + t + 1)
                    nc.vector.bn_aggr(mv[:, t], stats[:, t]).then_inc(mv_done, 1)

            def moments2(b, t):
                dve.wait_ge(x2_done, NT * b + t + 1)
                nc.vector.bn_stats(stats2[:, t], x_sb[:, b, t]).then_inc(stats2_done, 1)

            def residual(b, t):
                dve.wait_ge(attn_ready, NT * b + t + 1)
                nc.vector.scalar_tensor_tensor(out=x_sb[:, b, t], in0=ps_e[t][:], scalar=1.0 / (LN_SCALE * PROB_SCALE),
                                               in1=x_sb[:, b, t], op0=ALU.mult, op1=ALU.add).then_inc(x2_done, 1)

            def aggregate2(b):
                for t in range(NT):
                    dve.wait_ge(stats2_done, NT * b + t + 1)
                    nc.vector.bn_aggr(mv2[:, t], stats2[:, t]).then_inc(mv2_done, 1)

            def abs_rows(m):
                dve.wait_ge(abs_done, NCH * (m + 1))
                nc.vector.tensor_reduce(abs_row[:, m:m + 1], abs_sum[:, m], AX.X, ALU.add).then_inc(abs_row_done, 1)

            def quantiser_scale(m):
                dve.wait_ge(abs_all_done, m + 1)
                nc.vector.tensor_scalar(scale[:, m:m + 1], abs_all[:, m:m + 1], 1.0 / (F * D), QUANT_EPS,
                                        ALU.mult, ALU.max).then_inc(scale_done, 1)
                dve.wait_ge(scale_done, m + 1)
                nc.vector.reciprocal(inv_scale[:, m:m + 1], scale[:, m:m + 1]).then_inc(inv_scale_done, 1)

            def quantise(m, c):
                n = NCH * m + c
                src, dst = chunk_views(m, c)
                w_out, t_out = (whole[:], tern[:]) if m == 0 else (whole[:].bitcast(BF16), tern[:].bitcast(BF16))
                dve.wait_ge(rounded, n + 1)
                if n:
                    dve.wait_ge(tern_done, n)
                nc.vector.tensor_scalar(chunk_shape(m, w_out), src, ROUND, 1.0, ALU.subtract,
                                        ALU.min).then_inc(whole_done, 1)
                dve.wait_ge(whole_done, n + 1)
                if n:
                    dve.wait_ge(turned_done, n)
                nc.vector.tensor_scalar(t_out, w_out, -1.0, None, ALU.max).then_inc(tern_done, 1)
                dve.wait_ge(tern_done, n + 1)
                if m == 0:
                    flat = t_out.rearrange("p (q n r) -> p q n r", q=Q, r=R)
                else:
                    flat = t_out.rearrange("p (e k c) -> p e k c", k=2, c=R)
                nc.vector.transpose(dst, flat).then_inc(turned_done, 1)

            def step(b):
                low_ln(xnT_hi_done, b, XN_ORDER, lambda j: xnT[:, 0, j], lambda j: xnT[:, 1, j])
                for c in W1_PLAN[b][0]:
                    quantise(0, c)
                low_probs(b)
                if b == 1:
                    quantiser_scale(0)
                if b == LAST:
                    quantiser_scale(1)
                if b < LAST:
                    maxima(b + 1)
                if b > 0:
                    low_ln(x2T_hi_done, b - 1, range(ND), lambda j: x2T[:, 0, b - 1, j],
                           lambda j: x2T[:, 1, b - 1, j])
                if b < LAST:
                    inverse(b + 1, NT - 2)
                    inverse(b + 1, NT - 1)
                    if b + 1 < BY_ACT:
                        moments(b + 1)
                for t in range(NT):
                    for c in W1_PLAN[b][1 + t]:
                        quantise(0, c)
                    residual(b, t)
                    if t:
                        moments2(b, t - 1)
                moments2(b, NT - 1)
                aggregate2(b)
                if b == 0:
                    abs_rows(0)
                if b == LAST - 1:
                    abs_rows(1)

            def low_gelus(b, g, tiles=range(4)):
                for t in tiles:
                    dve.wait_ge(gT_hi_done, NF * b + 4 * g + t + 1)
                    nc.vector.scalar_tensor_tensor(out=gT_lo[:, 4 * g + t], in0=ps_t[t][:],
                                                   scalar=h_scale[:, bass.ds(4 * g + t, 1)], in1=gT_hi[:, 4 * g + t],
                                                   op0=ALU.mult, op1=ALU.subtract).then_inc(bank_read[t], 1)

            def results(b):
                for t in range(NT):
                    dve.wait_ge(y_ready, NT * b + t + 1)
                    dve.wait_ge(b2_added, NT * b + t + 1)
                    nc.vector.tensor_tensor(x_sb[:, b, t], ps_e[t][:], x_sb[:, b, t], ALU.add).then_inc(y_done, 1)

            nc.vector.memset(minus_half[:], -0.5).then_inc(minus_half_done, 1)
            moments(0)
            dve.wait_ge(b1T_ready, 1)
            nc.vector.tensor_copy(b1_col[:], ps_t[3][:, 0:NF]).then_inc(bank_read[3], 1)
            dve.wait_ge(bank_read[3], 1)
            nc.vector.tensor_scalar(bound[:].bitcast(I32), b1_col[:].bitcast(I32), 0x7FFFFFFF, None,
                                    ALU.bitwise_and).then_inc(bound_step, 1)
            dve.wait_ge(bound_step, 1)
            nc.vector.tensor_scalar(bound[:], bound[:], float(D + 1), None, ALU.add).then_inc(bound_step, 1)
            dve.wait_ge(bound_step, 2)
            nc.vector.tensor_scalar(bound[:].bitcast(I32), bound[:].bitcast(I32), 0x7F800000, None,
                                    ALU.bitwise_and).then_inc(bound_step, 1)
            dve.wait_ge(bound_step, 3)
            nc.vector.tensor_scalar(h_unscale[:], bound[:], 1.0 / HIDDEN_TOP, None, ALU.mult).then_inc(bound_step, 1)
            dve.wait_ge(bound_step, 4)
            nc.vector.reciprocal(h_scale[:], h_unscale[:]).then_inc(h_scale_done, 1)
            maxima(0)
            inverse(0, NT - 2)
            inverse(0, NT - 1)
            for b in range(B):
                step(b)
            for g in range(GROUPS):
                for half in range(2):
                    low_gelus(0, g, (2 * half, 2 * half + 1))
                    quantise(1, 2 * g + half)
            results(0)
            low_ln(x2T_hi_done, LAST, range(ND), lambda j: x2T[:, 0, LAST, j], lambda j: x2T[:, 1, LAST, j])
            with dve.Fori(1, B) as b:
                with dve.Fori(0, GROUPS) as g:
                    low_gelus(b, g)
                results(b)


_INS = ["x", "ctx_1024", "L0_xattn_Wq", "L0_xattn_bq", "L0_xattn_Wk", "L0_xattn_bk",
        "L0_ffn_w1", "L0_ffn_b1", "L0_ffn_w2", "L0_ffn_b2"]


def kernel(**inputs):
    import numpy as np
    import concourse.bacc as bacc
    from concourse.bass_utils import run_bass_kernel_spmd

    nc = bacc.Bacc("TRN2", target_bir_lowering=False, num_devices=1)
    arrays, args = {}, []
    for name in _INS:
        a = np.ascontiguousarray(inputs[name])
        arrays[f"in_{name}"] = a
        args.append(nc.dram_tensor(f"in_{name}", a.shape, mybir.dt.from_np(a.dtype), kind="ExternalInput").ap())
    shape = arrays["in_x"].shape
    out = nc.dram_tensor("out", shape, F32, kind="ExternalOutput").ap()
    xattn_ffn(nc, *args, out)
    r = run_bass_kernel_spmd(nc, [arrays], core_ids=[0])
    return r.results[0]["out"]
```

```python
from contextlib import ExitStack

import concourse.bass as bass
from concourse import mybir
from concourse.alu_op_type import AluOpType as ALU

ACT = mybir.ActivationFunctionType
AX = mybir.AxisListType
F32 = mybir.dt.float32
F16 = mybir.dt.float16
BF16 = mybir.dt.bfloat16
U8 = mybir.dt.uint8
I32 = mybir.dt.int32
U32 = mybir.dt.uint32

LN_SCALE = 2.0 ** 10
PROB_SCALE = 2.0 ** 15
HIDDEN_TOP = 2.0 ** 14
LN_EPS = 1e-5
QUANT_EPS = 1e-8
WARM_UP = 10
ROUND = 1.5 * 2.0 ** 23


def xattn_ffn(nc, x, ctx_in, Wq, bq, Wk, bk, w1, b1, w2, b2, out):
    B, L, D = x.shape
    C = ctx_in.shape[2]
    H = Wq.shape[0]
    F = w1.shape[0]
    P = 128
    NT = L // P
    NC = C // P
    ND = D // P
    NF = F // P
    Q = 4
    R = P // Q
    NCH = 8
    WN = F * D // P
    CH = WN // NCH
    assert ctx_in.shape[1] == L and D == L and H == P and D == ND * P

    with ExitStack() as stack:
        def sb(name, shape, dt=F32):
            return stack.enter_context(nc.sbuf_tensor(name, shape, dt))

        def sem(name):
            return stack.enter_context(nc.semaphore(name))

        x_sb = sb("x_sb", [P, B, NT, D])
        w1_raw = sb("w1_raw", [P, F // R, P])
        w2_raw = sb("w2_raw", [P, D // R, F // Q])
        w1T = sb("w1T", [P, NF, ND // 2, P, 2], F16)
        x2T = sb("x2T", [P, 2, B, ND, L], F16)
        scratch = sb("scratch", [P, 2, NT, D])
        probs = scratch[:, 0]
        xn = scratch[:, 1]
        x2n = sb("x2n", [P, NT, ND // 2, P, 2])
        W_raw = x2n[:, 0:2].rearrange("p a b c s -> p a (b c s)")[:, :, 0:C]
        W_columns = W_raw.rearrange("p s (i k) -> p s k i", k=NC)
        ctx_sb = sb("ctx_sb", [P, L // R, C // Q])
        ctxT = sb("ctxT", [P, NC, L])
        qkT = sb("qkT", [P, 2, L])
        WT = sb("WT", [P, 2, NC, H])
        xnT = sb("xnT", [P, 2, ND, L], F16)
        probsT = sb("probsT", [P, 2, NT, L], F16)
        tern = sb("tern", [P, 2, CH], F16)
        abs_out = sb("abs_out", [P, CH], U8)
        x_out = sb("x_out", [P, D], U8)
        b2_sb = sb("b2_sb", [P, D])
        ident = sb("ident", [P, P])
        b1_rows = sb("b1_rows", [NF, P])
        b1_col = sb("b1_col", [P, NF])
        bqk = sb("bqk", [P, 2])
        h_scale = sb("h_scale", [P, NF])
        h_unscale = sb("h_unscale", [P, NF])
        bound = sb("bound", [P, NF])
        abs_sum = sb("abs_sum", [P, 2, NCH])
        abs_row = sb("abs_row", [P, 2])
        abs_all = sb("abs_all", [P, 2])
        scale = sb("scale", [P, 2])
        inv_scale = sb("inv_scale", [P, 2])
        stats = sb("stats", [P, NT, 6])
        mv = sb("mv", [P, NT, 2])
        var_eps = sb("var_eps", [P, NT])
        neg_mean = sb("neg_mean", [P, NT])
        xsum = sb("xsum", [P, NT])
        xsquare = sb("xsquare", [P, NT])
        rstd = sb("rstd", [P, NT])
        stats2 = sb("stats2", [P, NT, 6])
        mv2 = sb("mv2", [P, NT, 2])
        var_eps2 = sb("var_eps2", [P, NT])
        neg_mean2 = sb("neg_mean2", [P, NT])
        rstd2 = sb("rstd2", [P, NT])
        minus_half = sb("minus_half", [P, NT])
        row_max = sb("row_max", [P, NT])
        row_sum = sb("row_sum", [P, NT])
        row_inv = sb("row_inv", [P, NT])

        w1_flat = w1_raw[:].rearrange("p a b -> p (a b)")
        w2T = w1_flat[:, 0:WN // 2].bitcast(BF16).rearrange("p (k e) -> p k e", k=NF)
        gT_hi = w1_flat[:, WN // 2:WN].bitcast(F16).rearrange("p (k t) -> p k t", k=NF)
        gT_lo = scratch[:].rearrange("p a b c -> p (a b c)").bitcast(F16).rearrange("p (k t) -> p k t", k=NF)

        ps_t = [stack.enter_context(nc.psum_tensor(f"ps_t{i}", [P, L], F32)) for i in range(4)]
        ps_e = [stack.enter_context(nc.psum_tensor(f"ps_e{i}", [P, L], F32)) for i in range(4)]

        W_here, b1_here, bqk_here = sem("W_here"), sem("b1_here"), sem("bqk_here")
        ctx_here = sem("ctx_here")
        x_here = sem("x_here")
        w_here = [[sem(f"w{m + 1}_here{h}") for h in range(2)] for m in range(2)]
        b2_here, out_done = sem("b2_here"), sem("out_done")
        ident_zero, ident_done = sem("ident_zero"), sem("ident_done")
        neg_mean_done = sem("neg_mean_done")
        ln_step, rstd_done, xn_done = sem("ln_step"), sem("rstd_done"), sem("xn_done")
        ln2_step, rstd2_done, x2n_done = sem("ln2_step"), sem("rstd2_done"), sem("x2n_done")
        scaled, rounded = sem("scaled"), sem("rounded")
        probs_done = sem("probs_done")
        b2_added = sem("b2_added")
        abs_all_done = sem("abs_all_done")
        WT_ready, b1T_ready = sem("WT_ready"), sem("b1T_ready")
        ctxT_ready, qk_ready, scores_ready = sem("ctxT_ready"), sem("qk_ready"), sem("scores_ready")
        xnT_ready, probsT_ready, attn_ready = sem("xnT_ready"), sem("probsT_ready"), sem("attn_ready")
        x2T_ready, hidden_ready, y_ready = sem("x2T_ready"), sem("hidden_ready"), sem("y_ready")
        WT_done, qkT_done = sem("WT_done"), sem("qkT_done")
        exp_done, abs_done = sem("exp_done"), sem("abs_done")
        xsum_done, xsquare_done = sem("xsum_done"), sem("xsquare_done")
        probsT_hi_done, xnT_hi_done, x2T_hi_done = sem("probsT_hi_done"), sem("xnT_hi_done"), sem("x2T_hi_done")
        gelu_done, gT_hi_done = sem("gelu_done"), sem("gT_hi_done")
        stats_done, mv_done = sem("stats_done"), sem("mv_done")
        stats2_done, mv2_done = sem("stats2_done"), sem("mv2_done")
        max_done, inv_done, x2_done, y_done = sem("max_done"), sem("inv_done"), sem("x2_done"), sem("y_done")
        abs_row_done, scale_done, inv_scale_done = sem("abs_row_done"), sem("scale_done"), sem("inv_scale_done")
        tern_done, turned_done = sem("tern_done"), sem("turned_done")
        bound_step, h_scale_done, w2T_done = sem("bound_step"), sem("h_scale_done"), sem("w2T_done")
        b1_col_done = sem("b1_col_done")
        minus_half_done, zeros_done = sem("minus_half_done"), sem("zeros_done")
        bank_read = [sem(f"bank_read{j}") for j in range(4)]

        LAST = B - 1

        def n_xn(b):
            return 3 * b - 1 if b else 0

        def n_probs(b):
            return n_xn(b) + 1

        def n_x2(b):
            return n_probs(b + 1) + 1 if b < LAST else AFTER_A + GROUPS

        AFTER_A = n_probs(LAST) + 2
        GROUPS = NF // 4

        def n_hidden(b, g):
            first = isinstance(b, int) and b == 0
            return AFTER_A + g if first else AFTER_A + GROUPS * b + 1 + g

        BY_DVE = 2
        BY_ACT = 3


        W1_PLAN = [[[], [], [], [], []], [[], [], [], [], []], [[], [0, 1], [2], [], []], [[], [3, 4], [5], [6], [7]]]

        def chunk_views(m, c):
            if m == 0:
                src = w1_raw[:].rearrange("p (q k) e -> p q k e", q=Q)[:, :, 2 * c:2 * c + 2]
                dst = w1T[:, 2 * c:2 * c + 2].rearrange("p k h f s -> p (k h f s)").bitcast(U32).rearrange(
                    "p (k h q r) -> p q (k h) r", k=2, h=ND // 2, q=Q)
            else:
                src = w2_raw[:].rearrange("p e (k c) -> p e k c", c=R)[:, :, 2 * c:2 * c + 2]
                dst = w2T[:, 2 * c:2 * c + 2].rearrange("p k (e r) -> p e k r", r=R)
            return src, dst

        def whole_view(m, c):
            src, _ = chunk_views(m, c)
            return src.bitcast(F16 if m == 0 else BF16)[:, :, :, 0:src.shape[-1]]

        def chunk_shape(m, flat):
            if m == 0:
                return flat.rearrange("p (q k e) -> p q k e", q=Q, k=2)
            return flat.rearrange("p (e k c) -> p e k c", k=2, c=R)

        HALVES = (slice(0, D // 2), slice(D // 2, D))
        LAST_BANKS = (ps_e[NT - 1], ps_e[0])
        X2_AFTER = [1] * LAST + [NT - 2]

        x_tiles = x.rearrange("b (t p) d -> b p t d", p=P)
        ctx_view = ctx_in.rearrange("b (tb r) (q c) -> b q r tb c", r=R, q=Q)
        out_tiles = out.rearrange("b (t p) d -> b p t d", p=P)
        w_views = [w1.rearrange("(fb r) (q d) -> q r fb d", r=R, q=Q), w2.rearrange("(eb r) (q f) -> q r eb f", r=R, q=Q)]
        b1_view = b1.rearrange("(q k c) -> k q c", q=Q, k=NF)
        raws = [w1_raw, w2_raw]

        block = stack.enter_context(nc.Block())

        @block.sync
        def _(sp):
            def load_ctx(b):
                if b:
                    sp.wait_ge(ctxT_ready, b)
                for q in range(Q):
                    sp.dma_start(ctx_sb[q * R:(q + 1) * R], ctx_view[b, q]).then_inc(ctx_here, 16)

            def load_x(b):
                if b:
                    sp.wait_ge(x_here, 16 * b)
                sp.dma_start(x_sb[:, b], x_tiles[b]).then_inc(x_here, 16)

            def load_w(m, h):
                n = raws[m].shape[1] // 2
                for q in range(Q):
                    sp.dma_start(raws[m][q * R:(q + 1) * R, h * n:(h + 1) * n, :],
                                 w_views[m][q, :, h * n:(h + 1) * n, :]).then_inc(w_here[m][h], 16)

            load_ctx(0)
            load_x(0)
            sp.dma_start(bqk[:, 0:1], bq.rearrange("(p a) -> p a", a=1)).then_inc(bqk_here, 16)
            sp.dma_start(bqk[:, 1:2], bk.rearrange("(p a) -> p a", a=1)).then_inc(bqk_here, 16)
            load_ctx(1)
            load_x(1)
            load_w(0, 0)
            load_ctx(2)
            load_w(0, 1)
            load_x(2)
            load_ctx(3)
            load_x(3)
            load_w(1, 0)
            sp.dma_start(b2_sb[:], b2.rearrange("(a d) -> a d", a=1).to_broadcast([P, D])).then_inc(b2_here, 16)
            load_w(1, 1)

            def store(b, tiles):
                for t in tiles:
                    sp.wait_ge(y_done, NT * b + t + 1)
                    sp.dma_start(out_tiles[b, :, t], x_sb[:, b, t]).then_inc(out_done, 16)

            with sp.Fori(0, LAST) as b:
                store(b, range(NT))
            store(LAST, range(NT - 1))
            for n, columns in enumerate(HALVES):
                sp.wait_ge(y_done, NT * B + n)
                sp.dma_start(out_tiles[LAST, :, NT - 1, columns], x_sb[:, LAST, NT - 1, columns]).then_inc(out_done, 16)
            sp.wait_ge(out_done, 16 * (B * NT + 1))

        @block.gpsimd
        def _(pool):
            def inverse_std(b, mv_t, ready, ve, nm, step_done, r, r_done):
                pool.wait_ge(ready, NT * b + NT)
                nc.gpsimd.tensor_scalar(ve[:], mv_t[:, :, 1], LN_EPS, None, ALU.add).then_inc(step_done, 1)
                nc.gpsimd.tensor_scalar(nm[:], mv_t[:, :, 0], -1.0, None, ALU.mult).then_inc(step_done, 1)
                pool.wait_ge(step_done, 2 * b + 2)
                nc.gpsimd.tensor_tensor(r[:], ve[:], minus_half[:], ALU.pow).then_inc(r_done, 1)
                pool.wait_ge(r_done, b + 1)

            def mean_of_sums(b):
                pool.wait_ge(xsum_done, NT * (b - BY_ACT + 1))
                nc.gpsimd.tensor_scalar(neg_mean[:], xsum[:], -1.0 / D, 1.0, ALU.mult, ALU.mult).then_inc(neg_mean_done, 1)

            def inverse_std_of_sums(b):
                n = b - BY_ACT
                pool.wait_ge(xsquare_done, NT * (n + 1))
                nc.gpsimd.tensor_scalar(var_eps[:], xsquare[:], 1.0 / D, LN_EPS, ALU.mult, ALU.add).then_inc(ln_step, 1)
                pool.wait_ge(ln_step, 2 * BY_ACT + n + 1)
                nc.gpsimd.tensor_tensor(rstd[:], var_eps[:], minus_half[:], ALU.pow).then_inc(rstd_done, 1)
                pool.wait_ge(rstd_done, b + 1)

            def layernorm(b):
                if b < BY_ACT:
                    inverse_std(b, mv, mv_done, var_eps, neg_mean, ln_step, rstd, rstd_done)
                else:
                    inverse_std_of_sums(b)
                if b:
                    pool.wait_ge(xnT_ready, ND * b)
                for t in range(NT if b else BY_DVE):
                    nc.gpsimd.tensor_scalar(xn[:, t], x_sb[:, b, t], neg_mean[:, t:t + 1], rstd[:, t:t + 1],
                                            ALU.add, ALU.mult).then_inc(xn_done, 1)

            def layernorm2(b):
                inverse_std(b, mv2, mv2_done, var_eps2, neg_mean2, ln2_step, rstd2, rstd2_done)
                if b:
                    pool.wait_ge(x2T_ready, ND * b)
                else:
                    pool.wait_ge(WT_ready, 1)
                for t in range(NT):
                    nc.gpsimd.tensor_scalar(x2n[:, t].rearrange("p h (q c) s -> p q h (c s)", q=Q),
                                            x_sb[:, b, t].rearrange("p (q h c) -> p q h c", q=Q, h=ND // 2),
                                            neg_mean2[:, t:t + 1], rstd2[:, t:t + 1],
                                            ALU.add, ALU.mult).then_inc(x2n_done, 1)

            def normalise_probs(b):
                for t in range(NT):
                    pool.wait_ge(inv_done, NT * b + t + 1)
                    nc.gpsimd.tensor_scalar(probs[:, t], probs[:, t], row_inv[:, t:t + 1], PROB_SCALE,
                                            ALU.mult, ALU.mult).then_inc(probs_done, 1)

            def add_b2(b):
                if b == 0:
                    pool.wait_ge(b2_here, 16)
                for t in range(NT):
                    pool.wait_ge(x2n_done, NT * b + t + 1)
                    nc.gpsimd.tensor_tensor(x_sb[:, b, t], x_sb[:, b, t], b2_sb[:], ALU.add).then_inc(b2_added, 1)

            def weight_total(m):
                pool.wait_ge(abs_row_done, m + 1)
                nc.gpsimd.partition_all_reduce(abs_all[:, m:m + 1], abs_row[:, m:m + 1], P,
                                               bass.bass_isa.ReduceOp.add).then_inc(abs_all_done, 1)

            def round_weights(m, chunks):
                pool.wait_ge(inv_scale_done, m + 1)
                for c in chunks:
                    src, _ = chunk_views(m, c)
                    nc.gpsimd.tensor_scalar(src, src, inv_scale[:, m:m + 1], ROUND, ALU.mult,
                                            ALU.add).then_inc(scaled, 1)
                    pool.wait_ge(scaled, NCH * m + c + 1)
                    nc.gpsimd.tensor_scalar(whole_view(m, c), src, -ROUND, 1.0, ALU.add,
                                            ALU.mult).then_inc(rounded, 1)

            def unscale(c):
                pool.wait_ge(turned_done, NCH + c + 1)
                for k in (2 * c, 2 * c + 1):
                    nc.gpsimd.tensor_scalar(w2T[:, k], w2T[:, k], h_unscale[:, k:k + 1], 1.0,
                                            ALU.mult, ALU.mult).then_inc(w2T_done, 1)

            nc.gpsimd.memset(ident[:], 0.0).then_inc(ident_zero, 1)
            pool.wait_ge(ident_zero, 1)
            nc.gpsimd.affine_select(out=ident[:], in_=ident[:], compare_op=ALU.not_equal, fill=1.0, base=0,
                                    pattern=[[-1, P]], channel_multiplier=1).then_inc(ident_done, 1)
            pool.wait_ge(minus_half_done, 1)
            layernorm(0)
            normalise_probs(0)
            for b in range(B):
                if BY_ACT <= b + 1 < B:
                    mean_of_sums(b + 1)
                if b < LAST:
                    normalise_probs(b + 1)
                if b == 1:
                    weight_total(0)
                if b < LAST:
                    layernorm(b + 1)
                if b == 1:
                    round_weights(0, (0, 1, 2, 3))
                elif b == 2:
                    round_weights(0, (4, 5, 6, 7))
                elif b == LAST:
                    weight_total(1)
                    round_weights(1, range(NCH))
                layernorm2(b)
            for c in range(NCH):
                unscale(c)
            for b in range(B):
                add_b2(b)

        @block.tensor
        def _(pe):
            def project(b, e_free):
                pe.wait_ge(ctxT_ready, b + 1)
                for s in range(2):
                    e_free(s)
                    for k in range(NC):
                        mm = nc.tensor.matmul(ps_e[s][:], WT[:, s, k], ctxT[:, k], start=(k == 0), stop=(k == NC - 1))
                    mm.then_inc(qk_ready, 1)

            def scores(b, e_free):
                pe.wait_ge(qkT_done, 2 * b + 2)
                for t in range(NT):
                    if t >= 2:
                        e_free(t)
                    nc.tensor.matmul(ps_e[t][:], qkT[:, 0, t * P:(t + 1) * P], qkT[:, 1], start=True,
                                     stop=True).then_inc(scores_ready, 1)

            def turn_probs(b):
                pe.wait_ge(probs_done, NT * b + NT)
                for j in range(NT):
                    pe.wait_ge(bank_read[j], n_probs(b))
                    for t in range(NT):
                        mm = nc.tensor.transpose(ps_t[j][:, t * P:(t + 1) * P], probs[:, t, j * P:(j + 1) * P], ident[:])
                    mm.then_inc(probsT_ready, 1)

            def turn_xn(b):
                pe.wait_ge(xn_done, NT * b + NT)
                for j in range(ND):
                    if b:
                        pe.wait_ge(bank_read[j], n_xn(b))
                    for t in range(NT):
                        mm = nc.tensor.transpose(ps_t[j][:, t * P:(t + 1) * P], xn[:, t, j * P:(j + 1) * P], ident[:])
                    mm.then_inc(xnT_ready, 1)

            def turn_x2n(b):
                pe.wait_ge(x2n_done, NT * b + NT)
                for j in range(ND):
                    pe.wait_ge(bank_read[j], n_x2(b))
                    for t in range(NT):
                        mm = nc.tensor.transpose(ps_t[j][:, t * P:(t + 1) * P], x2n[:, t, j // 2, :, j % 2], ident[:])
                    mm.then_inc(x2T_ready, 1)

            def attend(b, free, tiles=range(NT)):
                for t in tiles:
                    free(t)
                    for n, (u, v) in enumerate(((0, 0), (0, 1), (1, 0))):
                        for j in range(NT):
                            if t == 0 and n == 0:
                                if j == 0:
                                    pe.wait_ge(xnT_hi_done, ND * b + ND)
                                pe.wait_ge(probsT_hi_done, NT * b + j + 1)
                            if t == 0 and n == 1:
                                pe.wait_ge(bank_read[j], n_probs(b) + 1)
                            if t == 0 and n == 2:
                                pe.wait_ge(bank_read[j], n_xn(b) + 1)
                            mm = nc.tensor.matmul(ps_e[t][:], xnT[:, u, j, t * P:(t + 1) * P], probsT[:, v, j],
                                                  start=(n == 0 and j == 0), stop=(n == 2 and j == NT - 1))
                    mm.then_inc(attn_ready, 1)

            def step(b):
                def e_free(t):
                    if b:
                        pe.wait_ge(x2_done, NT * b - NT + t + 1)
                    else:
                        pe.wait_ge(exp_done, t + 1)

                turn_xn(b)
                if b < LAST:
                    project(b + 1, e_free)
                turn_probs(b)
                if b < LAST:
                    scores(b + 1, e_free)

                    def e_free(t):
                        pe.wait_ge(exp_done, NT * b + NT + t + 1)
                attend(b, e_free, range(X2_AFTER[b] + 1))
                if b > 0:
                    turn_x2n(b - 1)
                attend(b, e_free, range(X2_AFTER[b] + 1, NT))

            def hidden(b, g, first_weights=False):
                for t in range(4):
                    if first_weights and t % 2 == 0:
                        pe.wait_ge(turned_done, 2 * g + t // 2 + 1)
                    pe.wait_ge(bank_read[t], n_hidden(b, g))
                    for v in range(2):
                        for j in range(ND):
                            mm = nc.tensor.matmul(ps_t[t][:], w1T[:, g * 4 + t, j // 2, :, j % 2], x2T[:, v, b, j],
                                                  start=(v == 0 and j == 0), stop=(v == 1 and j == ND - 1))
                    mm.then_inc(hidden_ready, 1)

            def output(b, free, first_weights=False, tiles=range(NT)):
                for t in tiles:
                    free(t)
                    for k in range(NF):
                        if t == 0 and first_weights:
                            pe.wait_ge(w2T_done, k + 1)
                        if t == 0:
                            pe.wait_ge(bank_read[k % 4], n_hidden(b, k // 4) + 1)
                        for part in (gT_hi, gT_lo):
                            mm = nc.tensor.matmul(ps_e[t][:], part[:, k, t * P:(t + 1) * P], w2T[:, k],
                                                  start=(k == 0 and part is gT_hi), stop=(k == NF - 1 and part is gT_lo))
                    mm.then_inc(y_ready, 1)

            def last_output():
                for half, columns in enumerate(HALVES):
                    pe.wait_ge(y_done, NT * LAST + half)
                    for k in range(NF):
                        for part in (gT_hi, gT_lo):
                            mm = nc.tensor.matmul(LAST_BANKS[half][:, columns], part[:, k, (NT - 1) * P:NT * P],
                                                  w2T[:, k, columns], start=(k == 0 and part is gT_hi),
                                                  stop=(k == NF - 1 and part is gT_lo))
                    mm.then_inc(y_ready, 1)

            pe.wait_ge(zeros_done, 1)
            for _ in range(WARM_UP):
                nc.tensor.matmul(ps_e[0][:], tern[:, 0, 0:P], tern[:, 0, 0:L], start=True, stop=True)
            pe.wait_ge(ident_done, 1)
            pe.wait_ge(W_here, 16 * 2)
            for s in range(2):
                for k in range(NC):
                    mm = nc.tensor.transpose(ps_e[2][:, (2 * s + k) * P:(2 * s + k + 1) * P],
                                             W_columns[:, s, k], ident[:])
            mm.then_inc(WT_ready, 1)
            pe.wait_ge(b1_here, 16)
            nc.tensor.transpose(ps_e[3][:, 0:NF], b1_rows[:], ident[0:NF, 0:NF]).then_inc(b1T_ready, 1)
            pe.wait_ge(WT_done, 1)
            project(0, lambda s: None)
            scores(0, lambda t: pe.wait_ge(b1_col_done, 1))

            for b in range(B):
                step(b)

            with pe.Fori(0, GROUPS) as g:
                hidden(0, g, first_weights=True)
            output(0, lambda t: pe.wait_ge(x2_done, NT * LAST + t + 1), first_weights=True)
            turn_x2n(LAST)
            with pe.Fori(1, LAST) as b:
                with pe.Fori(0, GROUPS) as g:
                    hidden(b, g)
                output(b, lambda t: pe.wait_ge(y_done, NT * b - NT + t + 1))
            with pe.Fori(0, GROUPS) as g:
                hidden(LAST, g)
            output(LAST, lambda t: pe.wait_ge(y_done, NT * LAST - NT + t + 1), tiles=range(NT - 1))
            last_output()

        @block.scalar
        def _(act):
            def copy_qk(b):
                for s in range(2):
                    act.wait_ge(qk_ready, 2 * b + s + 1)
                    nc.scalar.activation(qkT[:, s], ps_e[s][:], ACT.Identity,
                                         bias=bqk[:, s:s + 1]).then_inc(qkT_done, 1)

            def exps(b):
                for t in range(NT):
                    act.wait_ge(max_done, NT * b + t + 1)
                    nc.scalar.activation(probs[:, t], ps_e[t][:], ACT.Exp, bias=row_max[:, t:t + 1],
                                         accum_out=row_sum[:, t:t + 1]).then_inc(exp_done, 1)

            def high_probs(b):
                for j in range(NT):
                    act.wait_ge(probsT_ready, NT * b + j + 1)
                    nc.scalar.copy(probsT[:, 0, j], ps_t[j][:]).then_inc(probsT_hi_done, 1)

            def high_ln(ready, b, dst, done):
                for j in range(ND):
                    act.wait_ge(ready, ND * b + j + 1)
                    nc.scalar.mul(dst(j), ps_t[j][:], LN_SCALE).then_inc(done, 1)

            def sum_x(b):
                act.wait_ge(x_here, 16 * b + 16)
                if b > BY_ACT:
                    act.wait_ge(xsquare_done, NT * (b - BY_ACT))
                for t in range(NT):
                    if t:
                        act.wait_ge(xsum_done, NT * (b - BY_ACT) + t)
                    nc.scalar.activation(x_out[:], x_sb[:, b, t], ACT.Identity,
                                         accum_out=xsum[:, t:t + 1]).then_inc(xsum_done, 1)

            def sum_squares(b):
                act.wait_ge(neg_mean_done, b - BY_ACT + 1)
                for t in range(NT):
                    if t:
                        act.wait_ge(xsquare_done, NT * (b - BY_ACT) + t)
                    nc.scalar.activation(x_out[:], x_sb[:, b, t], ACT.Square, bias=neg_mean[:, t:t + 1],
                                         accum_out=xsquare[:, t:t + 1]).then_inc(xsquare_done, 1)

            def sum_abs(m, chunks=range(NCH)):
                flat = raws[m][:].rearrange("p a b -> p (a b)")
                for c in chunks:
                    if c % (NCH // 2) == 0:
                        act.wait_ge(w_here[m][c // (NCH // 2)], 16 * Q)
                    if m or c:
                        act.wait_ge(abs_done, NCH * m + c)
                    nc.scalar.activation(abs_out[:], flat[:, c * CH:(c + 1) * CH], ACT.Abs,
                                         accum_out=abs_sum[:, m, c:c + 1]).then_inc(abs_done, 1)

            def step(b):
                high_ln(xnT_ready, b, lambda j: xnT[:, 0, j], xnT_hi_done)
                if b == 1:
                    sum_abs(0, (4, 5, 6))
                if BY_ACT <= b + 1 < B:
                    sum_x(b + 1)
                if b < LAST:
                    copy_qk(b + 1)
                high_probs(b)
                if b == 1:
                    sum_abs(0, [7])
                if b < LAST:
                    exps(b + 1)
                if BY_ACT <= b + 1 < B:
                    sum_squares(b + 1)
                if b == LAST:
                    sum_abs(1, range(4, NCH))
                if b > 0:
                    high_ln(x2T_ready, b - 1, lambda j: x2T[:, 0, b - 1, j], x2T_hi_done)
                if b == 0:
                    sum_abs(0, range(4))
                elif b == 2:
                    sum_abs(1, range(4))

            def gelus(b, g):
                for pair in range(2):
                    for t in (2 * pair, 2 * pair + 1):
                        act.wait_ge(hidden_ready, NF * b + 4 * g + t + 1)
                        nc.scalar.activation(ps_t[t][:], ps_t[t][:], ACT.Gelu, scale=1.0 / LN_SCALE,
                                             bias=b1_col[:, bass.ds(4 * g + t, 1)]).then_inc(gelu_done, 1)
                    for t in (2 * pair, 2 * pair + 1):
                        act.wait_ge(gelu_done, NF * b + 4 * g + t + 1)
                        nc.scalar.activation(gT_hi[:, 4 * g + t], ps_t[t][:], ACT.Identity,
                                             scale=h_scale[:, bass.ds(4 * g + t, 1)]).then_inc(gT_hi_done, 1)

            act.dma_start(W_raw[:, 0, :], Wq).then_inc(W_here, 16)
            act.dma_start(W_raw[:, 1, :], Wk).then_inc(W_here, 16)
            act.dma_start(b1_rows[:].rearrange("k (q c) -> k q c", q=Q), b1_view).then_inc(b1_here, 16)
            act.wait_ge(WT_ready, 1)
            nc.scalar.copy(WT[:].rearrange("p s k h -> p (s k h)"), ps_e[2][:]).then_inc(WT_done, 1)
            act.wait_ge(bqk_here, 16 * 2)
            copy_qk(0)
            exps(0)
            for b in range(B):
                step(b)
            act.wait_ge(turned_done, NCH)
            act.wait_ge(h_scale_done, 1)
            gelus(0, 0)
            with act.Fori(1, GROUPS) as g:
                gelus(0, g)
            high_ln(x2T_ready, LAST, lambda j: x2T[:, 0, LAST, j], x2T_hi_done)
            with act.Fori(1, B) as b:
                with act.Fori(0, GROUPS) as g:
                    gelus(b, g)

        @block.vector
        def _(dve):
            def turn_ctx(b):
                dve.wait_ge(ctx_here, 16 * Q * (b + 1))
                if b:
                    dve.wait_ge(qk_ready, 2 * b)
                nc.vector.transpose(ctxT[:].rearrange("p k (tb r) -> p tb k r", r=R),
                                    ctx_sb[:].rearrange("p tb (c k) -> p tb k c", c=R)).then_inc(ctxT_ready, 1)

            def low_probs(b, tiles=range(NT)):
                for j in tiles:
                    dve.wait_ge(probsT_hi_done, NT * b + j + 1)
                    nc.vector.tensor_tensor(probsT[:, 1, j], ps_t[j][:], probsT[:, 0, j],
                                            ALU.subtract).then_inc(bank_read[j], 1)

            def low_ln(hi_done, b, hi, lo):
                for j in range(ND):
                    dve.wait_ge(hi_done, ND * b + j + 1)
                    nc.vector.scalar_tensor_tensor(out=lo(j), in0=ps_t[j][:], scalar=LN_SCALE, in1=hi(j),
                                                   op0=ALU.mult, op1=ALU.subtract).then_inc(bank_read[j], 1)

            def low_x2(b):
                low_ln(x2T_hi_done, b, lambda j: x2T[:, 0, b, j], lambda j: x2T[:, 1, b, j])

            def inverse(b, t):
                dve.wait_ge(exp_done, NT * b + t + 1)
                nc.vector.reciprocal(row_inv[:, t:t + 1], row_sum[:, t:t + 1]).then_inc(inv_done, 1)

            def maxima(b, tiles=range(NT)):
                for t in tiles:
                    dve.wait_ge(scores_ready, NT * b + t + 1)
                    nc.vector.tensor_reduce(row_max[:, t:t + 1], ps_e[t][:], AX.X, ALU.max,
                                            negate=True).then_inc(max_done, 1)
                    if t >= 2:
                        inverse(b, t - 2)

            def moments(b):
                dve.wait_ge(x_here, 16 * b + 16)
                for t in range(NT):
                    nc.vector.bn_stats(stats[:, t], x_sb[:, b, t]).then_inc(stats_done, 1)
                for t in range(NT):
                    dve.wait_ge(stats_done, NT * b + t + 1)
                    nc.vector.bn_aggr(mv[:, t], stats[:, t]).then_inc(mv_done, 1)

            def moments2(b, t):
                dve.wait_ge(x2_done, NT * b + t + 1)
                nc.vector.bn_stats(stats2[:, t], x_sb[:, b, t]).then_inc(stats2_done, 1)

            def residual(b, t):
                dve.wait_ge(attn_ready, NT * b + t + 1)
                nc.vector.scalar_tensor_tensor(out=x_sb[:, b, t], in0=ps_e[t][:], scalar=1.0 / (LN_SCALE * PROB_SCALE),
                                               in1=x_sb[:, b, t], op0=ALU.mult, op1=ALU.add).then_inc(x2_done, 1)

            def aggregate2(b):
                for t in range(NT):
                    dve.wait_ge(stats2_done, NT * b + t + 1)
                    nc.vector.bn_aggr(mv2[:, t], stats2[:, t]).then_inc(mv2_done, 1)

            def abs_rows(m):
                dve.wait_ge(abs_done, NCH * (m + 1))
                nc.vector.tensor_reduce(abs_row[:, m:m + 1], abs_sum[:, m], AX.X, ALU.add).then_inc(abs_row_done, 1)

            def quantiser_scale(m):
                dve.wait_ge(abs_all_done, m + 1)
                nc.vector.tensor_scalar(scale[:, m:m + 1], abs_all[:, m:m + 1], 1.0 / (F * D), QUANT_EPS,
                                        ALU.mult, ALU.max).then_inc(scale_done, 1)
                dve.wait_ge(scale_done, m + 1)
                nc.vector.reciprocal(inv_scale[:, m:m + 1], scale[:, m:m + 1]).then_inc(inv_scale_done, 1)

            def quantise(m, c):
                n = NCH * m + c
                _, dst = chunk_views(m, c)
                t_out = tern[:, n % 2] if m == 0 else tern[:, n % 2].bitcast(BF16)
                dve.wait_ge(rounded, n + 1)
                if n >= 2:
                    dve.wait_ge(turned_done, n - 1)
                nc.vector.tensor_scalar(chunk_shape(m, t_out), whole_view(m, c), -1.0, 1.0, ALU.max,
                                        ALU.min).then_inc(tern_done, 1)
                dve.wait_ge(tern_done, n + 1)
                if m == 0:
                    flat = t_out.bitcast(U32).rearrange("p (q n r) -> p q n r", q=Q, r=R)
                else:
                    flat = t_out.rearrange("p (e k c) -> p e k c", k=2, c=R)
                nc.vector.transpose(dst, flat).then_inc(turned_done, 1)

            def end_of_moments2(b):
                moments2(b, NT - 2)
                moments2(b, NT - 1)
                aggregate2(b)

            def step(b):
                low_ln(xnT_hi_done, b, lambda j: xnT[:, 0, j], lambda j: xnT[:, 1, j])
                if 0 < b < LAST:
                    end_of_moments2(b - 1)
                for c in W1_PLAN[b][0]:
                    quantise(0, c)
                low_probs(b, range(NT - 1))
                if b < LAST:
                    maxima(b + 1, [0])
                low_probs(b, [NT - 1])
                if b == LAST:
                    end_of_moments2(b - 1)
                if b < LAST:
                    maxima(b + 1, range(1, NT))
                    inverse(b + 1, NT - 2)
                    inverse(b + 1, NT - 1)
                    if b == 1:
                        abs_rows(0)
                    if b + 1 < BY_ACT:
                        moments(b + 1)
                    if b == 1:
                        turn_ctx(3)
                for t in range(NT):
                    for c in W1_PLAN[b][1 + t]:
                        quantise(0, c)
                    if b == 0 and t == NT - 1:
                        turn_ctx(2)
                    residual(b, t)
                    if b == 1 and t == 0:
                        scale_gelu()
                        quantiser_scale(0)
                    if b == LAST and t == 0:
                        abs_rows(1)
                    if b == LAST and t == 1:
                        quantiser_scale(1)
                    if b and t == X2_AFTER[b]:
                        low_x2(b - 1)
                    if 0 < t < NT - 1:
                        moments2(b, t - 1)

            def scale_gelu():
                dve.wait_ge(b1_col_done, 1)
                nc.vector.tensor_scalar(bound[:].bitcast(I32), b1_col[:].bitcast(I32), 0x7FFFFFFF, None,
                                        ALU.bitwise_and).then_inc(bound_step, 1)
                dve.wait_ge(bound_step, 1)
                nc.vector.tensor_scalar(bound[:], bound[:], float(D + 1), None, ALU.add).then_inc(bound_step, 1)
                dve.wait_ge(bound_step, 2)
                nc.vector.tensor_scalar(bound[:].bitcast(I32), bound[:].bitcast(I32), 0x7F800000, None,
                                        ALU.bitwise_and).then_inc(bound_step, 1)
                dve.wait_ge(bound_step, 3)
                nc.vector.tensor_scalar(h_unscale[:], bound[:], 1.0 / HIDDEN_TOP, None, ALU.mult).then_inc(bound_step, 1)
                dve.wait_ge(bound_step, 4)
                nc.vector.reciprocal(h_scale[:], h_unscale[:]).then_inc(h_scale_done, 1)

            def low_gelus(b, g, tiles=range(4)):
                for t in tiles:
                    dve.wait_ge(gT_hi_done, NF * b + 4 * g + t + 1)
                    nc.vector.scalar_tensor_tensor(out=gT_lo[:, 4 * g + t], in0=ps_t[t][:],
                                                   scalar=h_scale[:, bass.ds(4 * g + t, 1)], in1=gT_hi[:, 4 * g + t],
                                                   op0=ALU.mult, op1=ALU.subtract).then_inc(bank_read[t], 1)

            def results(b, tiles=range(NT)):
                for t in tiles:
                    dve.wait_ge(y_ready, NT * b + t + 1)
                    dve.wait_ge(b2_added, NT * b + t + 1)
                    nc.vector.tensor_tensor(x_sb[:, b, t], ps_e[t][:], x_sb[:, b, t], ALU.add).then_inc(y_done, 1)

            nc.vector.memset(tern[:, 0, 0:L], 0.0).then_inc(zeros_done, 1)
            nc.vector.memset(minus_half[:], -0.5).then_inc(minus_half_done, 1)
            turn_ctx(0)
            dve.wait_ge(b1T_ready, 1)
            nc.vector.tensor_copy(b1_col[:], ps_e[3][:, 0:NF]).then_inc(b1_col_done, 1)
            moments(0)
            turn_ctx(1)
            dve.wait_ge(rstd_done, 1)
            for t in range(BY_DVE, NT):
                nc.vector.tensor_scalar(xn[:, t], x_sb[:, 0, t], neg_mean[:, t:t + 1], rstd[:, t:t + 1],
                                        ALU.add, ALU.mult).then_inc(xn_done, 1)
            maxima(0)
            inverse(0, NT - 2)
            inverse(0, NT - 1)
            for b in range(B):
                step(b)
            quantise(1, 0)
            for c in range(1, NCH + 1):
                low_gelus(0, (c - 1) // 2, (0, 1) if c % 2 else (2, 3))
                if c < NCH:
                    quantise(1, c)
                if c == 2:
                    end_of_moments2(LAST)
            results(0)
            low_x2(LAST)
            with dve.Fori(1, LAST) as b:
                with dve.Fori(0, GROUPS) as g:
                    low_gelus(b, g)
                results(b)
            with dve.Fori(0, GROUPS) as g:
                low_gelus(LAST, g)
            results(LAST, range(NT - 1))
            for n, columns in enumerate(HALVES):
                dve.wait_ge(y_ready, NT * B + n)
                dve.wait_ge(b2_added, NT * B)
                nc.vector.tensor_tensor(x_sb[:, LAST, NT - 1, columns], LAST_BANKS[n][:, columns],
                                        x_sb[:, LAST, NT - 1, columns], ALU.add).then_inc(y_done, 1)


_INS = ["x", "ctx_1024", "L0_xattn_Wq", "L0_xattn_bq", "L0_xattn_Wk", "L0_xattn_bk",
        "L0_ffn_w1", "L0_ffn_b1", "L0_ffn_w2", "L0_ffn_b2"]


def kernel(**inputs):
    import numpy as np
    import concourse.bacc as bacc
    from concourse.bass_utils import run_bass_kernel_spmd

    nc = bacc.Bacc("TRN2", target_bir_lowering=False, num_devices=1)
    arrays, args = {}, []
    for name in _INS:
        a = np.ascontiguousarray(inputs[name])
        arrays[f"in_{name}"] = a
        args.append(nc.dram_tensor(f"in_{name}", a.shape, mybir.dt.from_np(a.dtype), kind="ExternalInput").ap())
    shape = arrays["in_x"].shape
    out = nc.dram_tensor("out", shape, F32, kind="ExternalOutput").ap()
    xattn_ffn(nc, *args, out)
    r = run_bass_kernel_spmd(nc, [arrays], core_ids=[0])
    return r.results[0]["out"]
```
